# Optimizing a Trainium2 kernel written in Bass

```python
import numpy as np
import jax
import jax.numpy as jnp

def _softmax(x, axis=-1):
    return jax.nn.softmax(x, axis=axis)

def _gelu(x):
    return jax.nn.gelu(x, approximate=True)

def _silu(x):
    return jax.nn.silu(x)

def _sigmoid(x):
    return jax.nn.sigmoid(x)

def _layernorm(x, axis=-1, eps=1e-05):
    m = jnp.mean(x, axis=axis, keepdims=True)
    v = jnp.var(x, axis=axis, keepdims=True)
    return (x - m) / jnp.sqrt(v + eps)

def _scatter_add(tgt, idx, src, axis=0):
    return tgt.at[idx].add(src)

def _segment_sum(src, seg, n):
    return jax.ops.segment_sum(src, seg, n)
kernel_name = 'mk_xattn_ffn_d1_seqx_r8_14cac1'

def setup_inputs(seed: int=0):
    np.random.seed(seed)
    _w = jnp.asarray

    def _rec_inputs():
        import jax
        import jax.numpy as jnp
        _rk = jax.random.key(seed)
        x = -0.0002928 + 1 * jax.random.normal(jax.random.fold_in(_rk, 1), (2, 256, 256), jnp.float32)
        _lenS = 256 - jax.random.randint(jax.random.fold_in(_rk, 7), (2,), 0, max(1, 256 // 4) + 1, jnp.int32)
        _lenS2 = 512 - jax.random.randint(jax.random.fold_in(_rk, 8), (2,), 0, max(1, 512 // 4) + 1, jnp.int32)
        _ctx_512P = jax.random.normal(jax.random.fold_in(_rk, 11), (2, 16, 64), jnp.float32)
        _ctx_512c = jax.random.dirichlet(jax.random.fold_in(_rk, 511), 0.3 * jnp.ones((16,), jnp.float32), (2, 512))
        _ctx_512t = jnp.einsum('bsk,bkd->bsd', _ctx_512c, _ctx_512P)
        _ctx_512t = _ctx_512t * jax.lax.rsqrt(jnp.mean(jnp.square(_ctx_512t)) + 1e-12) * 0.953939
        ctx_512 = 0.000227908 + 0.99994 * (_ctx_512t + 0.3 * jax.random.normal(jax.random.fold_in(_rk, 611), (2, 512, 64), jnp.float32))
        return (x, ctx_512)
    x, ctx_512 = _rec_inputs()

    def _L0_xattn_setup():
        import jax, jax.numpy as jnp
        import numpy as np
        B, S, L = (2, 128, 128)
        DIM_Q, H, K, D_C, D_CQ, R = (256, 16, 128, 64, 192, 64)

        def _rope_tables(seq_len, dim, dtype):
            inv_freq = 1.0 / 10000.0 ** (jnp.arange(0, dim, 2, dtype=dtype) / dim)
            t = jnp.arange(seq_len, dtype=dtype)
            freqs = t[:, None] * inv_freq[None, :]
            sin = jnp.repeat(jnp.sin(freqs), 2, axis=-1)
            cos = jnp.repeat(jnp.cos(freqs), 2, axis=-1)
            return (sin, cos)

        def _rotate_half(x):
            h = x.shape[-1] // 2
            return jnp.concatenate([-x[..., h:], x[..., :h]], axis=-1)
        key = jax.random.key(seed)
        ks = jax.random.split(key, 8)
        s_in = 1.0 / np.sqrt(DIM_Q)
        s_k = 1.0 / np.sqrt(K)
        s_cq = 1.0 / np.sqrt(D_CQ)
        s_c = 1.0 / np.sqrt(D_C)
        return {'hidden_q': jax.random.normal(ks[0], (B, S, DIM_Q), jnp.float32), 'kv_c': jax.random.normal(ks[1], (B, L, D_C), jnp.float32), 'Wq': jax.random.normal(ks[2], (H * K, DIM_Q), jnp.float32) * s_in, 'w_kc_q': jax.random.normal(ks[3], (H, K, D_CQ), jnp.float32) * s_k, 'w_kc_kv': jax.random.normal(ks[4], (H, K, D_C), jnp.float32) * s_k, 'W_qr': jax.random.normal(ks[5], (H, D_CQ, R), jnp.float32) * s_cq / np.sqrt(R), 'W_kr': jax.random.normal(ks[6], (H, D_C, R), jnp.float32) * s_c, 'Wo': jax.random.normal(ks[7], (DIM_Q, H * K), jnp.float32) * s_k}
    _L0_xattn_all = _L0_xattn_setup()
    _L0_xattn_in = {k: v for k, v in _L0_xattn_all.items() if k in ('Wq', 'w_kc_q', 'w_kc_kv', 'W_qr', 'W_kr', 'Wo')}
    del _L0_xattn_all

    def _L0_ffn_setup():
        import jax, jax.numpy as jnp
        import numpy as np
        NBITS = 4
        OUT_F = 256
        IN_F = 256

        def _bit_ste(w, nbits):
            step = float(2 ** nbits - 1)
            w = jnp.clip(w, -1.0, 1.0)
            return jnp.round(jnp.abs(w) * step) / step * jnp.sign(w)
        key = jax.random.key(seed)
        ks = jax.random.split(key, 6)
        ex = np.arange(NBITS - 1, -1, -1)
        exps = jnp.asarray(2.0 ** ex / (2.0 ** NBITS - 1), dtype=jnp.float32)
        inp = {'input': jax.random.normal(ks[0], (8, 256, IN_F), dtype=jnp.float32), 'pweight': jax.random.normal(ks[1], (OUT_F, IN_F, NBITS), dtype=jnp.float32), 'nweight': jax.random.normal(ks[2], (OUT_F, IN_F, NBITS), dtype=jnp.float32), 'exps': exps, 'bexps': exps, 'mask_weight': jnp.ones((NBITS,), dtype=jnp.float32), 'scale': jnp.array([0.05], dtype=jnp.float32), 'pbias': jax.random.uniform(ks[3], (OUT_F, NBITS), dtype=jnp.float32, minval=0.0, maxval=float(2 ** NBITS - 1)) // 1.0 % 2.0, 'nbias': jax.random.uniform(ks[4], (OUT_F, NBITS), dtype=jnp.float32, minval=0.0, maxval=float(2 ** NBITS - 1)) // 1.0 % 2.0, 'biasscale': jnp.array([0.05], dtype=jnp.float32)}
        return inp
    _L0_ffn_all = _L0_ffn_setup()
    _L0_ffn_in = {k: v for k, v in _L0_ffn_all.items() if k in ('pweight', 'nweight', 'exps', 'bexps', 'mask_weight', 'scale', 'pbias', 'nbias', 'biasscale')}
    del _L0_ffn_all
    return {'x': x, 'ctx_512': ctx_512, 'L0_xattn_Wq': _L0_xattn_in['Wq'], 'L0_xattn_w_kc_q': _L0_xattn_in['w_kc_q'], 'L0_xattn_w_kc_kv': _L0_xattn_in['w_kc_kv'], 'L0_xattn_W_qr': _L0_xattn_in['W_qr'], 'L0_xattn_W_kr': _L0_xattn_in['W_kr'], 'L0_xattn_Wo': _L0_xattn_in['Wo'], 'L0_ffn_pweight': _L0_ffn_in['pweight'], 'L0_ffn_nweight': _L0_ffn_in['nweight'], 'L0_ffn_exps': _L0_ffn_in['exps'], 'L0_ffn_bexps': _L0_ffn_in['bexps'], 'L0_ffn_mask_weight': _L0_ffn_in['mask_weight'], 'L0_ffn_scale': _L0_ffn_in['scale'], 'L0_ffn_pbias': _L0_ffn_in['pbias'], 'L0_ffn_nbias': _L0_ffn_in['nbias'], 'L0_ffn_biasscale': _L0_ffn_in['biasscale']}

def reference(x, ctx_512, L0_xattn_Wq, L0_xattn_w_kc_q, L0_xattn_w_kc_kv, L0_xattn_W_qr, L0_xattn_W_kr, L0_xattn_Wo, L0_ffn_pweight, L0_ffn_nweight, L0_ffn_exps, L0_ffn_bexps, L0_ffn_mask_weight, L0_ffn_scale, L0_ffn_pbias, L0_ffn_nbias, L0_ffn_biasscale):
    import jax
    import jax.numpy as jnp

    def _L0_xattn_ref(hidden_q, kv_c, Wq, w_kc_q, w_kc_kv, W_qr, W_kr, Wo):
        import jax, jax.numpy as jnp
        import numpy as np
        B, S, L = (2, 128, 128)
        DIM_Q, H, K, D_C, D_CQ, R = (256, 16, 128, 64, 192, 64)

        def _rope_tables(seq_len, dim, dtype):
            inv_freq = 1.0 / 10000.0 ** (jnp.arange(0, dim, 2, dtype=dtype) / dim)
            t = jnp.arange(seq_len, dtype=dtype)
            freqs = t[:, None] * inv_freq[None, :]
            sin = jnp.repeat(jnp.sin(freqs), 2, axis=-1)
            cos = jnp.repeat(jnp.cos(freqs), 2, axis=-1)
            return (sin, cos)

        def _rotate_half(x):
            h = x.shape[-1] // 2
            return jnp.concatenate([-x[..., h:], x[..., :h]], axis=-1)
        b, s, _ = hidden_q.shape
        l = kv_c.shape[1]
        q_hk = (hidden_q @ Wq.T).reshape(b, s, H, K)
        q_big = jnp.einsum('bshk,hkq->bshq', q_hk, w_kc_q)
        sin, cos = _rope_tables(l, D_C, kv_c.dtype)
        kv_rope = kv_c * cos[None] + _rotate_half(kv_c) * sin[None]
        q_r = jnp.einsum('bshq,hqr->bhsr', q_big, W_qr)
        k_r = jnp.einsum('bld,hdr->bhlr', kv_rope, W_kr)
        scores = jnp.einsum('bhsr,bhlr->bhsl', q_r, k_r)
        attn = jax.nn.softmax(scores, axis=-1)
        ctx_c = jnp.einsum('bhsl,bld->bhsd', attn, kv_rope)
        ctx_lat = jnp.einsum('bhsd,hkd->bshk', ctx_c, w_kc_kv)
        out = ctx_lat.reshape(b, s, H * K) @ Wo.T
        return out

    def _L0_ffn_ref(input, pweight, nweight, exps, bexps, mask_weight, scale, pbias, nbias, biasscale):
        import jax, jax.numpy as jnp
        import numpy as np
        NBITS = 4
        OUT_F = 256
        IN_F = 256

        def _bit_ste(w, nbits):
            step = float(2 ** nbits - 1)
            w = jnp.clip(w, -1.0, 1.0)
            return jnp.round(jnp.abs(w) * step) / step * jnp.sign(w)
        temp = 1.0
        mask = jax.nn.sigmoid(mask_weight)
        soft = jax.nn.sigmoid(temp * pweight) - jax.nn.sigmoid(temp * nweight)
        weight = jnp.einsum('oin,n->oi', soft, exps * mask) * scale[0]
        bias_raw = jnp.einsum('on,n->o', pbias - nbias, bexps)
        bias = _bit_ste(bias_raw, NBITS) * biasscale[0]
        return jnp.einsum('bsi,oi->bso', input, weight) + bias
    x = x + _L0_xattn_ref(_layernorm(x, axis=-1), ctx_512, L0_xattn_Wq, L0_xattn_w_kc_q, L0_xattn_w_kc_kv, L0_xattn_W_qr, L0_xattn_W_kr, L0_xattn_Wo)
    x = x + _L0_ffn_ref(_layernorm(x, axis=-1), L0_ffn_pweight, L0_ffn_nweight, L0_ffn_exps, L0_ffn_bexps, L0_ffn_mask_weight, L0_ffn_scale, L0_ffn_pbias, L0_ffn_nbias, L0_ffn_biasscale)
    return x

_drawn_inputs = setup_inputs


def setup_inputs(seed=0):
    import zlib

    import numpy as np

    out = dict(_drawn_inputs(seed))
    spreads = {'L0_ffn_mask_weight': (1.0, 0.6)}
    factors = {'L0_ffn_bexps': 5.742, 'L0_ffn_pbias': 5.432, 'L0_ffn_nbias': 5.738}
    for name, (base, spread) in spreads.items():
        noise = np.random.default_rng([zlib.crc32(name.encode()), seed]).standard_normal(out[name].shape)
        drawn = base * np.exp(spread * noise) if base else spread * noise
        out[name] = jnp.asarray(drawn.astype(out[name].dtype))
    for name, factor in factors.items():
        out[name] = (out[name] * factor).astype(out[name].dtype)
    return out
```

```python
from contextlib import ExitStack

import concourse.bass as bass
from concourse import mybir
from concourse.alu_op_type import AluOpType as ALU

import numpy as np

B, S, D = 2, 256, 256
L, DC = 512, 64
H, K, CQ, R = 16, 128, 192, 64
NB = 4
P = 128
TT = S // P
T = B * TT
LT = L // P
DT = D // P
NP = H // 2
QH = CQ // 2
TILES = B * 2 * TT
LAG = 3
EPS = 1e-5
LEVELS = float(2 ** NB - 1)
ROUND = 1.5 * 2.0 ** 23

Q1, WKT_, WOT_, CT_, N_, C_, V_, MT_, M_, Q0 = range(10)
STEPS = 10


def step_count(p, n):
    return STEPS * p + n


def q_count(p, b):
    return STEPS * p + STEPS - 1 + b


def xattn_ffn_kernel(nc, x, ctx_512, Wq, w_kc_q, w_kc_kv, W_qr, W_kr, Wo, pweight, nweight, exps, bexps,
                     mask_weight, scale, pbias, nbias, biasscale, rope_cos, rope_sin, out):
    f32 = mybir.dt.float32
    f32r = mybir.dt.float32r
    ACT = mybir.ActivationFunctionType
    AX = mybir.AxisListType.X

    x_dram = x.rearrange("b (t p) d -> p (b t) d", p=P)
    out_dram = out.rearrange("b (t p) d -> p (b t) d", p=P)
    ctx_dram = ctx_512.rearrange("b (t p) d -> p (b t) d", p=P)
    cos_dram = rope_cos.rearrange("(t p) d -> p t d", p=P)
    sin_dram = rope_sin.rearrange("(t p) d -> p t d", p=P)
    wq_dram = Wq.rearrange("(h k) d -> k h d", k=K)
    wk_dram = w_kc_q.rearrange("h k q -> k h q")
    wkv_dram = w_kc_kv.rearrange("h k d -> k h d")
    wqr_dram = W_qr.rearrange("h (q s) r -> q h (s r)", s=2)
    wo_dram = Wo.rearrange("(t o) k -> o t k", o=P)
    pw_dram = pweight.rearrange("(t o) i n -> o t (i n)", o=P)
    nw_dram = nweight.rearrange("(t o) i n -> o t (i n)", o=P)
    pb_dram = pbias.rearrange("(t o) n -> o t n", o=P)
    nb_dram = nbias.rearrange("(t o) n -> o t n", o=P)

    with ExitStack() as stack:
        def sb(name, shape, dt=f32):
            return stack.enter_context(nc.sbuf_tensor(name, shape, dt))

        def bank(name):
            return stack.enter_context(nc.psum_tensor(name, [P, 512], f32))

        def sem(name):
            return stack.enter_context(nc.semaphore(name))

        x_rows = sb("x_rows", [P, T, D])
        ctx_rows = sb("ctx_rows", [P, B * LT, DC])
        cos = sb("cos", [P, LT, DC])
        sin = sb("sin", [P, LT, DC])
        wq = sb("wq", [P, 2, D])
        wk = sb("wk", [P, 2, CQ])
        wkv = sb("wkv", [P, 2, DC])
        wqr = sb("wqr", [QH, 2, 2 * R])
        wkr = sb("wkr", [P, P])
        wo = sb("wo", [P, DT, 2 * K])
        pw = sb("pw", [P, DT, D * NB])
        nw = sb("nw", [P, DT, D * NB])
        pb = sb("pb", [P, DT, NB])
        nb = sb("nb", [P, DT, NB])
        bits = sb("bits", [P, 4, NB])
        mask_t = sb("mask_t", [P, NB])
        scales = sb("scales", [P, 2])
        ident = sb("ident", [P, P])
        neg_half = sb("neg_half", [P, T])
        stats = sb("stats", [P, T, 6])
        moments = sb("moments", [P, T, 2])
        var_eps = sb("var_eps", [P, T])
        rstd = sb("rstd", [P, T])
        xn = sb("xn", [P, T, D])
        hq_t = sb("hq_t", [P, DT, T * P])
        rot = sb("rot", [P, B * LT, DC])
        kv = sb("kv", [P, B * LT, 2 * DC])
        k_hi = sb("k_hi", [P, B, L], f32r)
        k_lo = sb("k_lo", [P, B, L], f32r)
        wk_t = sb("wk_t", [QH, 4, K])
        wo_t = sb("wo_t", [P, 2, D])
        wkr_c = sb("wkr_c", [P, 2 * P])
        c = sb("c", [P, 2 * R])
        v = sb("v", [P, D])
        m_t = sb("m_t", [P, D])
        m = sb("m", [P, DT, 2 * DC])
        q_hl = sb("q_hl", [P, 2 * B, S], f32r)
        n_all = sb("n_all", [P, NP, D])
        neg_max = sb("neg_max", [P, TILES])
        row_sum = sb("row_sum", [P, TILES])
        row_inv = sb("row_inv", [P, TILES])
        probs = sb("probs", [P, TILES, L])
        probs_t = sb("probs_t", [P, B, LT, 2, S])
        ctx_t = sb("ctx_t", [P, NP, T * P])
        w_ffn = sb("w_ffn", [P, DT, D])
        w_ffn_t = sb("w_ffn_t", [P, DT, D])
        b_raw = sb("b_raw", [P, DT])
        b_col = sb("b_col", [P, DT])
        b_rows = sb("b_rows", [P, D])
        x2 = sb("x2", [P, T, D])
        x2b = sb("x2b", [P, T, D])
        h_t = sb("h_t", [P, 2, D])
        y = sb("y", [P, T, D])

        score_bank = [bank("score0"), bank("score1")]
        trans_bank = [bank("trans0"), bank("trans1")]
        ctx_bank = bank("ctxb")
        work = [bank("work0"), bank("work1")]

        ld_x, ld_ctx, ld_rope, ld_small, ld_ffn = (sem("ld_" + s) for s in ("x", "ctx", "rope", "small", "ffn"))
        ld_wq, ld_wk, ld_wkv, ld_wqr, ld_wkr, ld_wo = (
            sem("ld_" + s) for s in ("wq", "wk", "wkv", "wqr", "wkr", "wo"))
        ident_made = sem("ident_made")
        zeros_made = sem("zeros_made")
        rstd_made = sem("rstd_made")
        dve_chain = sem("dve_chain")
        pool_chain = sem("pool_chain")
        act_chain = sem("act_chain")
        mask_made = sem("mask_made")
        var_made = sem("var_made")
        xn_made = sem("xn_made")
        hq_transposed = sem("hq_transposed")
        hq_taken = sem("hq_taken")
        kv_made = sem("kv_made")
        k_transposed = sem("k_transposed")
        k_hi_made = sem("k_hi_made")
        k_taken = sem("k_taken")
        work_made = sem("work_made")
        work_taken = sem("work_taken")
        q_hi_made = sem("q_hi_made")
        scored = sem("scored")
        max_made = sem("max_made")
        exp_made = sem("exp_made")
        inv_made = sem("inv_made")
        inv_seen = sem("inv_seen")
        norm_made = sem("norm_made")
        transposed = sem("transposed")
        probs_taken = sem("probs_taken")
        ctx_made = sem("ctx_made")
        ctx_taken = sem("ctx_taken")
        tanh_made = sem("tanh_made")
        ffn_w_made = sem("ffn_w_made")
        bias_made = sem("bias_made")
        ffn_w_transposed = sem("ffn_w_transposed")
        ffn_w_taken = sem("ffn_w_taken")
        bias_spread = sem("bias_spread")
        bias_taken = sem("bias_taken")
        attn_out = sem("attn_out")
        x2_made = sem("x2_made")
        h_transposed = sem("h_transposed")
        h_taken = sem("h_taken")
        ffn_out = sem("ffn_out")
        x2b_made = sem("x2b_made")
        y_made = sem("y_made")
        stored = sem("stored")

        block = stack.enter_context(nc.Block())

        @block.sync
        def _(sp):
            def pair_of(dram, p):
                return dram[:, bass.ds(2 * p, 2), :]

            def load_pair(p, first=False):
                def free(n):
                    if not first:
                        sp.wait_ge(work_made, step_count(p - 1, n))
                free(WKT_)
                sp.dma_start(wk[:], pair_of(wk_dram, p)).then_inc(ld_wk, 16)
                free(WOT_)
                sp.dma_start(wo[:], wo_dram[:, :, bass.ds(2 * K * p, 2 * K)]).then_inc(ld_wo, 16)
                free(CT_)
                sp.dma_start(wqr[:], pair_of(wqr_dram, p)).then_inc(ld_wqr, 16)
                if first:
                    sp.wait_ge(zeros_made, 1)
                for h in range(2):
                    sp.dma_start(wkr[64 * h:64 * h + 64, 64 * h:64 * h + 64],
                                 W_kr[bass.ds(2 * p + h, 1), :, :].rearrange("h d r -> (h d) r"))\
                      .then_inc(ld_wkr, 16)
                free(N_)
                sp.dma_start(wkv[:], pair_of(wkv_dram, p)).then_inc(ld_wkv, 16)
                free(V_)
                sp.dma_start(wq[:], pair_of(wq_dram, p)).then_inc(ld_wq, 16)

            sp.dma_start(x_rows[:], x_dram).then_inc(ld_x, 16)
            load_pair(0, first=True)
            sp.dma_start(pw[:], pw_dram).then_inc(ld_ffn, 16)
            sp.dma_start(nw[:], nw_dram).then_inc(ld_ffn, 16)
            with sp.Fori(1, NP) as p:
                load_pair(p)
            for t in range(T):
                sp.wait_ge(y_made, t + 1)
                sp.dma_start(out_dram[:, t, :], y[:, t, :]).then_inc(stored, 16)
            sp.wait_ge(stored, 16 * T)

        @block.gpsimd
        def _(pool):
            chain = [0]

            def link(instruction):
                chain[0] += 1
                instruction.then_inc(pool_chain, 1)
                pool.wait_ge(pool_chain, chain[0])

            pool.memset(wkr[:], 0.0).then_inc(zeros_made, 1)
            link(pool.memset(neg_half[:], -0.5))
            link(pool.memset(ident[:], 0.0))
            pool.affine_select(out=ident[:], in_=ident[:], compare_op=ALU.not_equal, fill=1.0, base=0,
                               pattern=[[-1, P]], channel_multiplier=1).then_inc(ident_made, 1)
            pool.wait_ge(var_made, 1)
            pool.tensor_tensor(rstd[:], var_eps[:], neg_half[:], ALU.pow).then_inc(rstd_made, 1)

            def normalise(t, j):
                pool.wait_ge(inv_made, t + 1)
                pool.sem_inc(inv_seen, 1)
                e = probs[:, j, :]
                pool.tensor_scalar(e, e, row_inv[:, j:j + 1], 1.0, ALU.mult, ALU.mult).then_inc(norm_made, 1)

            with pool.Fori(0, NP) as i:
                for j in range(TILES):
                    normalise(TILES * i + j, j)

            for t in range(T):
                pool.wait_ge(var_made, t + 2)
                pool.tensor_tensor(rstd[:, t:t + 1], var_eps[:, t:t + 1], neg_half[:, t:t + 1],
                                   ALU.pow).then_inc(rstd_made, 1)
                if t == 0:
                    pool.wait_ge(bias_taken, 1)
                pool.wait_ge(x2_made, t + 1)
                pool.tensor_tensor(x2b[:, t, :], x2[:, t, :], b_rows[:], ALU.add).then_inc(x2b_made, 1)

        @block.scalar
        def _(act):
            act.dma_start(ctx_rows[:], ctx_dram).then_inc(ld_ctx, 16)
            act.dma_start(cos[:], cos_dram).then_inc(ld_rope, 16)
            act.dma_start(sin[:], sin_dram).then_inc(ld_rope, 16)
            for n, vec in enumerate((exps, bexps, mask_weight)):
                act.dma_start(bits[:, n, :], vec.rearrange("(a n) -> a n", a=1).broadcast_to([P, NB])).then_inc(ld_small, 16)
            for n, vec in enumerate((scale, biasscale)):
                act.dma_start(scales[:, n:n + 1], vec.rearrange("(a n) -> a n", a=1).broadcast_to([P, 1]))\
                   .then_inc(ld_small, 16)
            act.dma_start(pb[:], pb_dram).then_inc(ld_small, 16)
            act.dma_start(nb[:], nb_dram).then_inc(ld_small, 16)

            act.wait_ge(ld_small, 16 * 7)
            act.activation(mask_t[:], bits[:, 2, :], ACT.Tanh, scale=0.5).then_inc(mask_made, 1)

            for n in range(DT):
                act.wait_ge(hq_transposed, n + 1)
                act.activation(hq_t[:, n, :], score_bank[n][:], ACT.Copy).then_inc(hq_taken, 1)
            for b in range(B):
                act.wait_ge(k_transposed, b + 1)
                act.activation(k_hi[:, b, :], trans_bank[b][:], ACT.Copy).then_inc(k_hi_made, 1)

            def q_high(count, b, g):
                act.wait_ge(work_made, count)
                for h in range(2):
                    last = act.activation(q_hl[0:64, 2 * b + h, :], g[64 * h:64 * h + 64, 0:S], ACT.Copy)
                last.then_inc(q_hi_made, 1)

            def exponentials(t, j):
                act.wait_ge(max_made, t + 1)
                act.activation(probs[:, j, :], score_bank[j % 2][:], ACT.Exp, bias=neg_max[:, j:j + 1],
                               accum_out=row_sum[:, j:j + 1]).then_inc(exp_made, 1)

            def take_transposed(t, j):
                act.wait_ge(transposed, t + 1)
                b, h, tt = j // (2 * TT), j // TT % 2, j % TT
                act.activation(probs_t[:, b, :, h, tt * P:tt * P + P],
                               trans_bank[j % 2][:].rearrange("p (l t) -> p l t", l=LT),
                               ACT.Copy).then_inc(probs_taken, 1)

            def one_pair(i, first=False, last=False):
                for j in range(TILES):
                    exponentials(TILES * i + j, j)
                    if j == 0:
                        q_high(q_count(i, 1), 1, work[Q1 % 2])
                    if j == 6 and not last:
                        q_high(q_count(i + 1, 0), 0, work[Q0 % 2])
                    if j >= LAG or not first:
                        take_transposed(TILES * i + j - LAG, (j - LAG) % TILES)
                    if last and 1 <= j <= 4:
                        if j == 1:
                            act.wait_ge(ld_ffn, 32)
                        w, ot = (pw, nw)[(j - 1) % 2], (j - 1) // 2
                        act.activation(w[:, ot, :], w[:, ot, :], ACT.Tanh, scale=0.5).then_inc(tanh_made, 1)

            q_high(q_count(0, 0), 0, work[Q0 % 2])
            one_pair(0, first=True)
            with act.Fori(1, NP - 1) as i:
                one_pair(i)
            one_pair(NP - 1, last=True)
            for j in range(TILES - LAG, TILES):
                take_transposed(TILES * (NP - 1) + j, j)
            act.wait_ge(ffn_w_transposed, 1)
            act.activation(w_ffn_t[:].rearrange("p t d -> p (t d)"), work[0][:], ACT.Copy).then_inc(ffn_w_taken, 1)
            for t in range(T):
                act.wait_ge(h_transposed, t + 1)
                act.activation(h_t[:, t % 2, :], trans_bank[t % 2][:, 0:D], ACT.Copy).then_inc(h_taken, 1)

        @block.vector
        def _(dve):
            chain = [0]

            def link(instruction):
                chain[0] += 1
                instruction.then_inc(dve_chain, 1)
                dve.wait_ge(dve_chain, chain[0])

            def norm_stats(rows, t):
                link(dve.bn_stats(stats[:, t, :], rows[:, t, :]))
                link(dve.bn_aggr(moments[:, t, :], stats[:, t, :]))

            def norm_apply(rows, t, count):
                dve.wait_ge(rstd_made, count)
                dve.tensor_scalar(xn[:, t, :], rows[:, t, :], moments[:, t, 0:1], rstd[:, t:t + 1],
                                  ALU.subtract, ALU.mult).then_inc(xn_made, 1)

            dve.wait_ge(ld_x, 16)
            for t in range(T):
                norm_stats(x_rows, t)
            dve.tensor_scalar(var_eps[:], moments[:, :, 1], EPS, None, ALU.add).then_inc(var_made, 1)

            dve.wait_ge(ld_ctx, 16)
            dve.wait_ge(ld_rope, 32)
            half = DC // 2
            for b in range(B):
                rows = slice(b * LT, b * LT + LT)
                dve.tensor_tensor(rot[:, rows, 0:half], ctx_rows[:, rows, half:DC], sin[:, :, 0:half], ALU.mult)
                link(dve.tensor_tensor(rot[:, rows, half:DC], ctx_rows[:, rows, 0:half], sin[:, :, half:DC],
                                       ALU.mult))
                link(dve.tensor_tensor(ctx_rows[:, rows, :], ctx_rows[:, rows, :], cos[:], ALU.mult))
                for side in range(2):
                    last = dve.tensor_tensor(kv[:, rows, side * DC:side * DC + DC], ctx_rows[:, rows, :],
                                             rot[:, rows, :], ALU.add)
                last.then_inc(kv_made, 1)
            for t in range(T):
                norm_apply(x_rows, t, 1)
            for b in range(B):
                dve.wait_ge(k_hi_made, b + 1)
                dve.tensor_tensor(k_lo[:, b, :], trans_bank[b][:], k_hi[:, b, :].bitcast(f32),
                                  ALU.subtract).then_inc(k_taken, 1)

            def take_step(p, n):
                g = work[n % 2]
                dve.wait_ge(work_made, step_count(p, n))
                to, what = {
                    WKT_: (wk_t[:].rearrange("q s k -> q (s k)"), g[0:QH, :]),
                    WOT_: (wo_t[:].rearrange("k h d -> k (h d)"), g[:]),
                    CT_: (wkr_c[:], g[:, 0:2 * P]),
                    N_: (n_all[:, bass.ds(p, 1), :].rearrange("q a d -> q (a d)"), g[:, 0:D]),
                    C_: (c[:], g[:, 0:P]),
                    V_: (v[:], g[:, 0:D]),
                    MT_: (m_t[:], g[:, 0:D]),
                    M_: (m[:].rearrange("q t d -> q (t d)"), g[:, 0:D]),
                }[n]
                dve.tensor_copy(to, what).then_inc(work_taken, 1)

            def q_low(p, b, g):
                dve.wait_ge(q_hi_made, 2 * p + b + 1)
                for h in range(2):
                    last = dve.tensor_tensor(q_hl[64:128, 2 * b + h, :], g[64 * h:64 * h + 64, 0:S],
                                             q_hl[0:64, 2 * b + h, :].bitcast(f32), ALU.subtract)
                last.then_inc(work_taken, 1)

            def maxima(t, j):
                dve.wait_ge(scored, t + 1)
                dve.tensor_reduce(neg_max[:, j:j + 1], score_bank[j % 2][:], axis=AX, op=ALU.max,
                                  negate=True).then_inc(max_made, 1)

            def inverses(t, j):
                dve.wait_ge(exp_made, t + 1)
                dve.reciprocal(row_inv[:, j:j + 1], row_sum[:, j:j + 1]).then_inc(inv_made, 1)

            def take_ctx(i, b):
                dve.wait_ge(ctx_made, B * i + b + 1)
                dve.tensor_copy(ctx_t[:, bass.ds(i, 1), b * S:b * S + S].rearrange("q a s -> q (a s)"),
                                ctx_bank[:, 0:S]).then_inc(ctx_taken, 1)

            def ffn_weights(j):
                if j == 0:
                    dve.wait_ge(mask_made, 1)
                    link(dve.tensor_scalar(bits[:, 3, :], mask_t[:], 0.5, 0.5, ALU.mult, ALU.add))
                    link(dve.tensor_tensor(bits[:, 3, :], bits[:, 3, :], bits[:, 0, :], ALU.mult))
                    link(dve.tensor_scalar(bits[:, 3, :], bits[:, 3, :], scales[:, 0:1], 0.5, ALU.mult, ALU.mult))
                if j == 1:
                    link(dve.tensor_tensor(pb[:], pb[:], nb[:], ALU.subtract))
                    for t in range(DT):
                        last = dve.tensor_tensor(pb[:, t, :], pb[:, t, :], bits[:, 1, :], ALU.mult)
                    link(last)
                    link(dve.tensor_reduce(b_raw[:], pb[:], axis=AX, op=ALU.add))
                    link(dve.tensor_scalar(b_raw[:], b_raw[:], -1.0, 1.0, ALU.max, ALU.min))
                    link(dve.tensor_scalar(b_raw[:], b_raw[:], LEVELS, ROUND, ALU.mult, ALU.add))
                    link(dve.tensor_scalar(b_raw[:], b_raw[:], -ROUND, 1.0 / LEVELS, ALU.add, ALU.mult))
                    dve.tensor_scalar(b_col[:], b_raw[:], scales[:, 1:2], None, ALU.mult).then_inc(bias_made, 1)
                if j in (3, 5):
                    ot = (j - 3) // 2
                    dve.wait_ge(tanh_made, 2 * ot + 2)
                    link(dve.tensor_tensor(pw[:, ot, :], pw[:, ot, :], nw[:, ot, :], ALU.subtract))
                if j in (4, 6):
                    ot = (j - 4) // 2
                    w_bits = pw[:, ot, :].rearrange("o (i n) -> o i n", n=NB)
                    link(dve.tensor_scalar(w_ffn[:, ot, :], w_bits[:, :, 0], bits[:, 3, 0:1], None, ALU.mult))
                    for n in range(1, NB):
                        last = dve.scalar_tensor_tensor(w_ffn[:, ot, :], w_bits[:, :, n], bits[:, 3, n:n + 1],
                                                        w_ffn[:, ot, :], ALU.mult, ALU.add)
                        if n < NB - 1:
                            link(last)
                    last.then_inc(ffn_w_made, 1)

            def one_pair(i, first=False, last=False):
                for j in range(TILES):
                    maxima(TILES * i + j, j)
                    if j == 0:
                        q_low(i, 1, work[Q1 % 2])
                    if not last:
                        if j in (1, 2):
                            take_step(i + 1, (WOT_, N_)[j - 1])
                        if j == 6:
                            q_low(i + 1, 0, work[Q0 % 2])
                    if j >= 1 or not first:
                        inverses(TILES * i + j - 1, (j - 1) % TILES)
                    if not last and j < 6:
                        take_step(i + 1, (WKT_, CT_, C_, V_, MT_, M_)[j])
                    if j == LAG and not first:
                        take_ctx(i - 1, 1)
                    if j == 4 + LAG:
                        take_ctx(i, 0)
                    if last:
                        ffn_weights(j)

            for n in range(WKT_, Q0):
                take_step(0, n)
            q_low(0, 0, work[Q0 % 2])
            one_pair(0, first=True)
            with dve.Fori(1, NP - 1) as i:
                one_pair(i)
            one_pair(NP - 1, last=True)
            inverses(TILES * NP - 1, TILES - 1)
            dve.wait_ge(bias_spread, 1)
            dve.tensor_copy(b_rows[:], work[1][:, 0:D]).then_inc(bias_taken, 1)
            take_ctx(NP - 1, 1)

            def residual(t):
                dve.wait_ge(attn_out, t + 1)
                dve.tensor_tensor(x2[:, t, :], score_bank[t % 2][:, 0:D], x_rows[:, t, :], ALU.add)\
                   .then_inc(x2_made, 1)
                dve.wait_ge(x2_made, t + 1)
                norm_stats(x2, t)
                dve.tensor_scalar(var_eps[:, t:t + 1], moments[:, t, 1:2], EPS, None, ALU.add)\
                   .then_inc(var_made, 1)
                norm_apply(x2, t, t + 2)

            def finish(t):
                dve.wait_ge(ffn_out, t + 1)
                dve.wait_ge(x2b_made, t + 1)
                dve.tensor_tensor(y[:, t, :], work[t % 2][:, 0:D], x2b[:, t, :], ALU.add).then_inc(y_made, 1)

            residual(0)
            for t in range(1, T):
                residual(t)
                finish(t - 1)
            finish(T - 1)

        @block.tensor
        def _(pe):
            pe.wait_ge(ident_made, 1)
            for b in range(B):
                pe.wait_ge(kv_made, b + 1)
                for lt in range(LT):
                    last = pe.transpose(trans_bank[b][:, lt * P:lt * P + P], kv[:, b * LT + lt, :], ident[:])
                last.then_inc(k_transposed, 1)
            pe.wait_ge(xn_made, T)
            for n in range(DT):
                for t in range(T):
                    last = pe.transpose(score_bank[n][:, t * P:t * P + P], xn[:, t, n * P:n * P + P], ident[:])
                last.then_inc(hq_transposed, 1)

            def prepare(p, n, first=False):
                g = work[n % 2]
                needs_last = n in (V_, MT_, M_)
                if not (first and n < 3) or needs_last:
                    pe.wait_ge(work_taken, step_count(p, n) - (1 if needs_last else 2))
                if n == WKT_:
                    pe.wait_ge(ld_wk, 16 * (p + 1))
                    for h in range(2):
                        for s in range(2):
                            last = pe.transpose(g[0:QH, (2 * h + s) * K:(2 * h + s + 1) * K], wk[:, h, s::2],
                                                ident[:])
                elif n == WOT_:
                    pe.wait_ge(ld_wo, 16 * (p + 1))
                    for h in range(2):
                        for t in range(DT):
                            last = pe.transpose(g[:, h * D + t * P:h * D + t * P + P], wo[:, t, h * K:h * K + K],
                                                ident[:])
                elif n == CT_:
                    pe.wait_ge(ld_wkr, 32 * (p + 1))
                    pe.transpose(g[:, 0:P], wkr[:], ident[:])
                    pe.wait_ge(ld_wqr, 16 * (p + 1))
                    for s in range(2):
                        for h in range(2):
                            last = pe.matmul(g[64 * h:64 * h + 64, P:P + K], wqr[:, h, s * R:s * R + R],
                                             wk_t[:, 2 * h + s, :], start=(s == 0), stop=(s == 1))
                elif n == N_:
                    pe.wait_ge(ld_wkv, 16 * (p + 1))
                    for h in range(2):
                        last = pe.matmul(g[64 * h:64 * h + 64, 0:D], wkv[:, h, :], wo_t[:, h, :],
                                         start=True, stop=True)
                elif n == C_:
                    last = pe.transpose(g[:, 0:P], wkr_c[:, P:2 * P], ident[:])
                elif n == V_:
                    pe.wait_ge(ld_wq, 16 * (p + 1))
                    for h in range(2):
                        last = pe.matmul(g[64 * h:64 * h + 64, 0:D], c[:, h * R:h * R + R], wq[:, h, :],
                                         start=True, stop=True)
                elif n == MT_:
                    last = pe.matmul(g[:, 0:D], wkr_c[:, 0:P], v[:], start=True, stop=True)
                elif n == M_:
                    for t in range(DT):
                        last = pe.transpose(g[:, t * P:t * P + P], m_t[:, t * P:t * P + P], ident[:])
                last.then_inc(work_made, 1)

            def queries(p, b, n):
                pe.wait_ge(work_taken, q_count(p, b) - 1)
                for t in range(DT):
                    last = pe.matmul(work[n % 2][:, 0:S], m[:, t, :], hq_t[:, t, b * S:b * S + S],
                                     start=(t == 0), stop=(t == DT - 1))
                last.then_inc(work_made, 1)

            def scores(i, t, j):
                b, h, tt = j // (2 * TT), j // TT % 2, j % TT
                if j % (2 * TT) == 0:
                    pe.wait_ge(work_taken, q_count(i, b))
                pe.wait_ge(exp_made, t - 1)
                q = q_hl[:, 2 * b + h, tt * P:tt * P + P]
                pe.matmul(score_bank[j % 2][:], q, k_hi[:, b, :], start=True, stop=False)
                pe.matmul(score_bank[j % 2][:], q, k_lo[:, b, :], start=False, stop=True).then_inc(scored, 1)

            def transpose_probs(t, j, fresh=False):
                pe.wait_ge(norm_made, t + 1)
                if not fresh:
                    pe.wait_ge(probs_taken, t - 1)
                for lt in range(LT):
                    last = pe.transpose(trans_bank[j % 2][:, lt * P:lt * P + P],
                                        probs[:, j, lt * P:lt * P + P], ident[:])
                last.then_inc(transposed, 1)

            def contexts(i, b, fresh=False):
                pe.wait_ge(probs_taken, TILES * i + 2 * TT * (b + 1))
                if not fresh:
                    pe.wait_ge(ctx_taken, B * i + b)
                for lt in range(LT):
                    for h in range(2):
                        last = pe.matmul(ctx_bank[64 * h:64 * h + 64, 0:S],
                                         kv[:, b * LT + lt, h * DC:h * DC + DC], probs_t[:, b, lt, h, :],
                                         start=(lt == 0), stop=(lt == LT - 1))
                last.then_inc(ctx_made, 1)

            def one_pair(i, first=False, last=False):
                for j in range(TILES):
                    t = TILES * i + j
                    if first and j == 0:
                        pe.wait_ge(k_taken, B)
                    if first and j < 2:
                        scores_first(j)
                    else:
                        scores(i, t, j)
                    if j == 0:
                        queries(i, 1, Q1)
                    if not last:
                        if j in (1, 2):
                            prepare(i + 1, (WOT_, N_)[j - 1])
                        if j == 6:
                            queries(i + 1, 0, Q0)
                    if j >= LAG or not first:
                        transpose_probs(t - LAG, (j - LAG) % TILES, fresh=first and j < LAG + 2)
                    if not last and j < 6:
                        prepare(i + 1, (WKT_, CT_, C_, V_, MT_, M_)[j])
                    if j == LAG and not first:
                        contexts(i - 1, 1)
                    if j == 4 + LAG:
                        contexts(i, 0, fresh=first)

            def scores_first(j):
                if j == 0:
                    pe.wait_ge(work_taken, q_count(0, 0))
                q = q_hl[:, 0, j * P:j * P + P]
                pe.matmul(score_bank[j][:], q, k_hi[:, 0, :], start=True, stop=False)
                pe.matmul(score_bank[j][:], q, k_lo[:, 0, :], start=False, stop=True).then_inc(scored, 1)

            for n in range(WKT_, Q0):
                prepare(0, n, first=True)
            pe.wait_ge(hq_taken, DT)
            queries(0, 0, Q0)
            one_pair(0, first=True)
            with pe.Fori(1, NP - 1) as i:
                one_pair(i)
            one_pair(NP - 1, last=True)

            for j in range(TILES - LAG, TILES - 1):
                transpose_probs(TILES * (NP - 1) + j, j)
            pe.wait_ge(ffn_w_made, DT)
            pe.wait_ge(work_taken, q_count(NP - 1, 1))
            for it in range(DT):
                for ot in range(DT):
                    last = pe.transpose(work[0][:, it * D + ot * P:it * D + ot * P + P],
                                        w_ffn[:, ot, it * P:it * P + P], ident[:])
            last.then_inc(ffn_w_transposed, 1)
            pe.wait_ge(bias_made, 1)
            for ot in range(DT):
                last = pe.matmul(work[1][:, ot * P:ot * P + P], b_col[:, ot:ot + 1].broadcast_to([P, P]), ident[:],
                                 start=True, stop=True)
            last.then_inc(bias_spread, 1)
            transpose_probs(TILES * NP - 1, TILES - 1)

            def project(t):
                if t >= 2:
                    pe.wait_ge(x2_made, t - 1)
                for p in range(NP):
                    last = pe.matmul(score_bank[t % 2][:, 0:D], ctx_t[:, p, t * P:t * P + P], n_all[:, p, :],
                                     start=(p == 0), stop=(p == NP - 1))
                last.then_inc(attn_out, 1)

            def ffn(t):
                pe.wait_ge(xn_made, T + t + 1)
                if t == 0:
                    pe.wait_ge(probs_taken, TILES * NP)
                if t >= 2:
                    pe.wait_ge(h_taken, t - 1)
                for n in range(DT):
                    last = pe.transpose(trans_bank[t % 2][:, n * P:n * P + P], xn[:, t, n * P:n * P + P], ident[:])
                last.then_inc(h_transposed, 1)
                pe.wait_ge(h_taken, t + 1)
                if t == 0:
                    pe.wait_ge(ffn_w_taken, 1)
                    pe.wait_ge(bias_taken, 1)
                if t >= 2:
                    pe.wait_ge(y_made, t - 1)
                for n in range(DT):
                    last = pe.matmul(work[t % 2][:, 0:D], h_t[:, t % 2, n * P:n * P + P], w_ffn_t[:, n, :],
                                     start=(n == 0), stop=(n == DT - 1))
                last.then_inc(ffn_out, 1)

            pe.wait_ge(ctx_taken, B * NP - 1)
            project(0)
            contexts(NP - 1, 1)
            project(1)
            pe.wait_ge(ctx_taken, B * NP)
            for t in range(2, T):
                ffn(t - 2)
                project(t)
            ffn(T - 2)
            ffn(T - 1)


_INS = ["x", "ctx_512", "L0_xattn_Wq", "L0_xattn_w_kc_q", "L0_xattn_w_kc_kv", "L0_xattn_W_qr", "L0_xattn_W_kr",
        "L0_xattn_Wo", "L0_ffn_pweight", "L0_ffn_nweight", "L0_ffn_exps", "L0_ffn_bexps", "L0_ffn_mask_weight",
        "L0_ffn_scale", "L0_ffn_pbias", "L0_ffn_nbias", "L0_ffn_biasscale"]


def rope_tables():
    f = np.float32
    inv_freq = f(1.0) / np.power(10000.0, np.arange(0, DC, 2) / DC).astype(f)
    angle = np.arange(L, dtype=f)[:, None] * inv_freq[None, :]
    sin = np.repeat(np.sin(angle), 2, axis=-1)
    cos = np.repeat(np.cos(angle), 2, axis=-1)
    sin[:, :DC // 2] = -sin[:, :DC // 2]
    return cos.astype(f), sin.astype(f)


def kernel(**inputs):
    import concourse.bacc as _bacc
    from concourse.bass_utils import run_bass_kernel_spmd as _run

    nc = _bacc.Bacc("TRN2", target_bir_lowering=False, num_devices=1)
    cos, sin = rope_tables()
    given = [(name, np.ascontiguousarray(inputs[name])) for name in _INS] + [("rope_cos", cos), ("rope_sin", sin)]
    arrays, args = {}, []
    for name, a in given:
        arrays[f"in_{name}_dram"] = a
        args.append(nc.dram_tensor(f"in_{name}_dram", a.shape, mybir.dt.from_np(a.dtype), kind="ExternalInput").ap())
    args.append(nc.dram_tensor("out_0_dram", (B, S, D), mybir.dt.float32, kind="ExternalOutput").ap())
    xattn_ffn_kernel(nc, *args)
    r = _run(nc, [arrays], core_ids=[0])
    return r.results[0]["out_0_dram"]
```

```python
from contextlib import ExitStack

import concourse.bass as bass
from concourse import mybir
from concourse.alu_op_type import AluOpType as ALU

import numpy as np

B, S, D = 2, 256, 256
L, DC = 512, 64
H, K, CQ, R = 16, 128, 192, 64
NB = 4
P = 128
TT = S // P
T = B * TT
LT = L // P
DT = D // P
NP = H // 2
QH = CQ // 2
BK = 32
TILES = B * 2 * TT
LAG = 3
EPS = 1e-5
LEVELS = float(2 ** NB - 1)
ROUND = 1.5 * 2.0 ** 23

N_, Q1, CT_, C_, V_, MT_, M_, Q0 = range(8)
STEPS = 8
SLOT_OF = {N_: 0, Q1: 1, CT_: 2, C_: 3, V_: 4, MT_: 5, M_: 6, Q0: 7}


def step_count(i, n):
    return STEPS * (i + 1) + n + 1 - CT_


def q_count(p, b):
    return step_count(p, Q1) if b else step_count(p - 1, Q0)


def slot_of(n, last):
    return 0 if last and n == Q1 else SLOT_OF[n]


def xattn_ffn_kernel(nc, x, ctx_512, Wq, w_kc_q, w_kc_kv, W_qr, W_kr, Wo, pweight, nweight, exps, bexps,
                     mask_weight, scale, pbias, nbias, biasscale, rope_table, out):
    f32 = mybir.dt.float32
    f32r = mybir.dt.float32r
    ACT = mybir.ActivationFunctionType
    AX = mybir.AxisListType.X

    x_dram = x.rearrange("b (t p) d -> p (b t) d", p=P)
    out_dram = out.rearrange("b (t p) d -> p (b t) d", p=P)
    ctx_dram = ctx_512.rearrange("b (t p) d -> p (b t) d", p=P)
    rope_dram = rope_table.rearrange("(t p) d -> p t d", p=P)
    wq_dram = Wq.rearrange("(h k) d -> k h d", k=K)
    wk_dram = w_kc_q.rearrange("h (i r) (s j c) -> j r s (h i) c", r=BK, s=2, c=BK)
    wkv_dram = w_kc_kv.rearrange("h k d -> k h d")
    wqr_dram = W_qr.rearrange("h (s q) r -> q (h s) r", s=2)
    wo_dram = Wo.rearrange("(i r) (h j c) -> j r h i c", r=BK, j=K // BK, c=BK)
    pw_dram = pweight.rearrange("(t o) i n -> o t (i n)", o=P)
    nw_dram = nweight.rearrange("(t o) i n -> o t (i n)", o=P)
    pb_dram = pbias.rearrange("(t o) n -> o t n", o=P)
    nb_dram = nbias.rearrange("(t o) n -> o t n", o=P)

    with ExitStack() as stack:
        def sb(name, shape, dt=f32):
            return stack.enter_context(nc.sbuf_tensor(name, shape, dt))

        def bank(name):
            return stack.enter_context(nc.psum_tensor(name, [P, 512], f32))

        def sem(name):
            return stack.enter_context(nc.semaphore(name))

        x_rows = sb("x_rows", [P, T, D])
        ctx_rows = sb("ctx_rows", [P, B * LT, DC])
        cos_sin = sb("cos_sin", [P, LT, 2 * DC])
        wq = sb("wq", [P, 2, D])
        wk = sb("wk", [QH, 2, 2 * K])
        wkv = sb("wkv", [P, 2, DC])
        wqr = sb("wqr", [QH, 4, R])
        wkr = sb("wkr", [P, P])
        wo = sb("wo", [P, 2, D])
        pw = sb("pw", [P, DT, D * NB])
        nw = sb("nw", [P, DT, D * NB])
        pb = sb("pb", [P, DT, NB])
        nb = sb("nb", [P, DT, NB])
        bits = sb("bits", [P, 4, NB])
        mask_t = sb("mask_t", [P, NB])
        scales = sb("scales", [P, 2])
        ident = sb("ident", [P, P])
        warm = sb("warm", [P, 1])
        neg_half = sb("neg_half", [P, T])
        stats = sb("stats", [P, T, 6])
        moments = sb("moments", [P, T, 2])
        var_eps = sb("var_eps", [P, T])
        rstd = sb("rstd", [P, T])
        xn = sb("xn", [P, T, D])
        hq_t = sb("hq_t", [P, B, DT, S])
        rot = sb("rot", [P, B * LT, DC])
        kv = sb("kv", [P, B * LT, 2 * DC])
        k_hi = sb("k_hi", [P, B, L], f32r)
        k_lo = sb("k_lo", [P, B, L], f32r)
        wk_t = sb("wk_t", [QH, 2, 2 * K])
        wo_t = sb("wo_t", [P, 2, D])
        wkr_c = sb("wkr_c", [P, 2 * P])
        c = sb("c", [P, 2 * R])
        v = sb("v", [P, D])
        m_t = sb("m_t", [P, D])
        m = sb("m", [P, DT, 2 * DC])
        q_hl = sb("q_hl", [P, 2 * B, S], f32r)
        n_all = sb("n_all", [P, NP, D])
        neg_max = sb("neg_max", [P, TILES])
        row_sum = sb("row_sum", [P, TILES])
        row_inv = sb("row_inv", [P, TILES])
        probs = sb("probs", [P, TILES, L])
        probs_t = sb("probs_t", [P, B, LT, 2, S])
        ctx_t = sb("ctx_t", [P, NP, T * P])
        w_ffn = sb("w_ffn", [P, DT, D])
        w_ffn_t = sb("w_ffn_t", [P, DT, D])
        b_raw = sb("b_raw", [P, DT])
        b_col = sb("b_col", [P, DT])
        b_rows = sb("b_rows", [P, D])
        x2 = sb("x2", [P, T, D])
        x2b = sb("x2b", [P, T, D])
        h_t = sb("h_t", [P, 2, D])
        y = sb("y", [P, T, D])

        score_bank = [bank("score0"), bank("score1")]
        trans_bank = [bank("trans0"), bank("trans1")]
        ctx_bank = bank("ctxb")
        work = [bank("work0"), bank("work1")]

        ld_rope, ld_small, ld_ffn = (sem("ld_" + s) for s in ("rope", "small", "ffn"))
        ld_x, ld_ctx = ([sem(f"ld_{s}{b}") for b in range(B)] for s in ("x", "ctx"))
        ld_wq, ld_wk, ld_wkv, ld_wqr, ld_wkr, ld_wo = (
            sem("ld_" + s) for s in ("wq", "wk", "wkv", "wqr", "wkr", "wo"))
        ident_made = sem("ident_made")
        zeros_made = sem("zeros_made")
        neg_half_made = sem("neg_half_made")
        rstd_made = sem("rstd_made")
        dve_chain = sem("dve_chain")
        pool_chain = sem("pool_chain")
        act_chain = sem("act_chain")
        mask_made = sem("mask_made")
        var_made = sem("var_made")
        xn_made = sem("xn_made")
        wk_turned = sem("wk_turned")
        wo_turned = sem("wo_turned")
        hq_transposed = sem("hq_transposed")
        hq_taken = sem("hq_taken")
        kv_made = [sem(f"kv_made{b}") for b in range(B)]
        k_transposed = sem("k_transposed")
        k_hi_made = sem("k_hi_made")
        k_taken = sem("k_taken")
        work_made = sem("work_made")
        work_taken = sem("work_taken")
        q_hi_made = sem("q_hi_made")
        scored = sem("scored")
        max_made = sem("max_made")
        exp_made = sem("exp_made")
        inv_made = sem("inv_made")
        inv_seen = sem("inv_seen")
        norm_made = sem("norm_made")
        transposed = sem("transposed")
        probs_taken = sem("probs_taken")
        ctx_made = sem("ctx_made")
        ctx_taken = sem("ctx_taken")
        tanh_made = sem("tanh_made")
        ffn_w_made = sem("ffn_w_made")
        bias_made = sem("bias_made")
        ffn_w_transposed = sem("ffn_w_transposed")
        ffn_w_taken = sem("ffn_w_taken")
        bias_spread = sem("bias_spread")
        bias_taken = sem("bias_taken")
        attn_out = sem("attn_out")
        x2_made = sem("x2_made")
        h_transposed = sem("h_transposed")
        h_taken = sem("h_taken")
        ffn_out = sem("ffn_out")
        x2b_made = sem("x2b_made")
        y_made = sem("y_made")
        stored = sem("stored")

        block = stack.enter_context(nc.Block())

        @block.sync
        def _(sp):
            def pair_of(dram, p):
                return dram[:, bass.ds(2 * p, 2), :]

            def load_queries_side(p, first=False):
                if not first:
                    sp.wait_ge(wk_turned, p)
                for j in range(QH // BK):
                    sp.dma_start(wk[j * BK:j * BK + BK, :, :].rearrange("r s (i c) -> r s i c", c=BK),
                                 wk_dram[j, :, :, bass.ds(8 * p, 8), :]).then_inc(ld_wk, 16)
                if not first:
                    sp.wait_ge(work_made, step_count(p - 2, CT_))
                sp.dma_start(wqr[:], wqr_dram[:, bass.ds(4 * p, 4), :]).then_inc(ld_wqr, 16)
                if first:
                    sp.wait_ge(zeros_made, 1)
                for h in range(2):
                    sp.dma_start(wkr[64 * h:64 * h + 64, 64 * h:64 * h + 64],
                                 W_kr[bass.ds(2 * p + h, 1), :, :].rearrange("h d r -> (h d) r"))\
                      .then_inc(ld_wkr, 16)
                if not first:
                    sp.wait_ge(work_made, step_count(p - 2, V_))
                sp.dma_start(wq[:], pair_of(wq_dram, p)).then_inc(ld_wq, 16)

            def load_values_side(p, first=False):
                if not first:
                    sp.wait_ge(wo_turned, p)
                for j in range(K // BK):
                    for h in range(2):
                        sp.dma_start(wo[j * BK:j * BK + BK, h, :].rearrange("r (i c) -> r i c", c=BK),
                                     wo_dram[j, :, bass.ds(2 * p + h, 1), :, :].rearrange("r h i c -> r (h i) c"))\
                          .then_inc(ld_wo, 16)
                if not first:
                    sp.wait_ge(work_made, step_count(p - 1, N_))
                sp.dma_start(wkv[:], pair_of(wkv_dram, p)).then_inc(ld_wkv, 16)

            load_queries_side(0, first=True)
            load_values_side(0, first=True)
            with sp.Fori(1, NP) as p:
                load_queries_side(p)
                load_values_side(p)
            for n, vec in enumerate((exps, bexps, mask_weight)):
                sp.dma_start(bits[:, n, :], vec.rearrange("(a n) -> a n", a=1).broadcast_to([P, NB]))\
                  .then_inc(ld_small, 16)
            for n, vec in enumerate((scale, biasscale)):
                sp.dma_start(scales[:, n:n + 1], vec.rearrange("(a n) -> a n", a=1).broadcast_to([P, 1]))\
                  .then_inc(ld_small, 16)
            sp.dma_start(pb[:], pb_dram).then_inc(ld_small, 16)
            sp.dma_start(nb[:], nb_dram).then_inc(ld_small, 16)
            sp.dma_start(pw[:], pw_dram).then_inc(ld_ffn, 16)
            sp.dma_start(nw[:], nw_dram).then_inc(ld_ffn, 16)
            for t in range(T):
                sp.wait_ge(y_made, t + 1)
                sp.dma_start(out_dram[:, t, :], y[:, t, :]).then_inc(stored, 16)
            sp.wait_ge(stored, 16 * T)

        def projected(t):
            return work[t // TT][:, t % TT * D:t % TT * D + D]

        def step_target(i, n):
            g = work[n % 2]
            if n == N_:
                return n_all[:, bass.ds(i, 1), :].rearrange("q a d -> q (a d)"), g[:, 0:D]
            return {
                CT_: (wkr_c[:], g[:, 0:2 * P]),
                C_: (c[:], g[:, 0:P]),
                V_: (v[:], g[:, 0:D]),
                MT_: (m_t[:], g[:, 0:D]),
                M_: (m[:].rearrange("q t d -> q (t d)"), g[:, 0:D]),
            }[n]

        def rope(eng, b, sem_of, count):
            half = DC // 2
            rows = slice(b * LT, b * LT + LT)

            def chained(instruction):
                count[0] += 1
                instruction.then_inc(sem_of, 1)
                eng.wait_ge(sem_of, count[0])

            eng.wait_ge(ld_ctx[b], 16)
            eng.tensor_tensor(rot[:, rows, 0:half], ctx_rows[:, rows, half:DC], cos_sin[:, :, DC:DC + half], ALU.mult)
            chained(eng.tensor_tensor(rot[:, rows, half:DC], ctx_rows[:, rows, 0:half], cos_sin[:, :, DC + half:2 * DC], ALU.mult))
            chained(eng.tensor_tensor(ctx_rows[:, rows, :], ctx_rows[:, rows, :], cos_sin[:, :, 0:DC], ALU.mult))
            for side in range(2):
                last = eng.tensor_tensor(kv[:, rows, side * DC:side * DC + DC], ctx_rows[:, rows, :],
                                         rot[:, rows, :], ALU.add)
            last.then_inc(kv_made[b], 1)

        @block.gpsimd
        def _(pool):
            chain = [0]

            def link(instruction):
                chain[0] += 1
                instruction.then_inc(pool_chain, 1)
                pool.wait_ge(pool_chain, chain[0])

            pool.memset(wkr[:], 0.0).then_inc(zeros_made, 1)
            pool.dma_start(cos_sin[:], rope_dram).then_inc(ld_rope, 16)
            pool.dma_start(ctx_rows[:, 0:LT, :], ctx_dram[:, 0:LT, :]).then_inc(ld_ctx[0], 16)
            pool.memset(neg_half[:], -0.5).then_inc(neg_half_made, 1)
            link(pool.memset(ident[:], 0.0))
            pool.affine_select(out=ident[:], in_=ident[:], compare_op=ALU.not_equal, fill=1.0, base=0,
                               pattern=[[-1, P]], channel_multiplier=1).then_inc(ident_made, 1)
            pool.wait_ge(neg_half_made, 1)
            for b in range(B):
                pool.wait_ge(var_made, b + 1)
                pool.tensor_tensor(rstd[:, b * TT:b * TT + TT], var_eps[:, b * TT:b * TT + TT],
                                   neg_half[:, 0:TT], ALU.pow).then_inc(rstd_made, 1)
            pool.wait_ge(ld_rope, 16)
            rope(pool, 1, pool_chain, chain)

            def normalise(t, j):
                pool.wait_ge(inv_made, t + 1)
                pool.sem_inc(inv_seen, 1)
                e = probs[:, j, :]
                pool.tensor_scalar(e, e, row_inv[:, j:j + 1], 1.0, ALU.mult, ALU.mult).then_inc(norm_made, 1)

            with pool.Fori(0, NP) as i:
                for j in range(TILES):
                    normalise(TILES * i + j, j)

            for pair in range(T // TT):
                tiles = range(pair * TT, pair * TT + TT)
                for t in tiles:
                    pool.wait_ge(var_made, B + t + 1)
                    pool.tensor_tensor(rstd[:, t:t + 1], var_eps[:, t:t + 1], neg_half[:, t:t + 1],
                                       ALU.pow).then_inc(rstd_made, 1)
                if pair == 0:
                    pool.wait_ge(bias_taken, 1)
                for t in tiles:
                    pool.wait_ge(x2_made, t + 1)
                    pool.tensor_tensor(x2b[:, t, :], x2[:, t, :], b_rows[:], ALU.add).then_inc(x2b_made, 1)

        @block.scalar
        def _(act):
            for b in range(B):
                act.dma_start(x_rows[:, b * TT:b * TT + TT, :], x_dram[:, b * TT:b * TT + TT, :])\
                   .then_inc(ld_x[b], 16)
            act.dma_start(ctx_rows[:, LT:2 * LT, :], ctx_dram[:, LT:2 * LT, :]).then_inc(ld_ctx[1], 16)
            act.wait_ge(neg_half_made, 1)
            act.activation(warm[:], neg_half[:, 0:1], ACT.Exp)

            def take_step(n):
                act.wait_ge(work_made, step_count(-1, n))
                to, what = step_target(-1, n)
                act.activation(to, what, ACT.Copy).then_inc(work_taken, 1)

            def take_hq(b):
                act.wait_ge(hq_transposed, b + 1)
                act.activation(hq_t[:, b, :, :].rearrange("p t s -> p (t s)"), score_bank[b][:], ACT.Copy)\
                   .then_inc(hq_taken, 1)

            def k_high(b):
                act.wait_ge(k_transposed, b + 1)
                act.activation(k_hi[:, b, :], trans_bank[b][:], ACT.Copy).then_inc(k_hi_made, 1)

            def q_high(count, b, g):
                act.wait_ge(work_made, count)
                for h in range(2):
                    last = act.activation(q_hl[0:64, 2 * b + h, :], g[64 * h:64 * h + 64, 0:S], ACT.Copy)
                last.then_inc(q_hi_made, 1)

            def exponentials(t, j):
                act.wait_ge(max_made, t + 1)
                act.activation(probs[:, j, :], score_bank[j % 2][:], ACT.Exp, bias=neg_max[:, j:j + 1],
                               accum_out=row_sum[:, j:j + 1]).then_inc(exp_made, 1)

            def take_transposed(t, j):
                act.wait_ge(transposed, t + 1)
                b, h, tt = j // (2 * TT), j // TT % 2, j % TT
                act.activation(probs_t[:, b, :, h, tt * P:tt * P + P],
                               trans_bank[j % 2][:].rearrange("p (l t) -> p l t", l=LT),
                               ACT.Copy).then_inc(probs_taken, 1)

            def one_pair(i, first=False, last=False):
                for j in range(TILES):
                    exponentials(TILES * i + j, j)
                    if j == slot_of(Q1, last):
                        q_high(q_count(i, 1), 1, work[Q1 % 2])
                    if j == SLOT_OF[Q0] and not last:
                        q_high(q_count(i + 1, 0), 0, work[Q0 % 2])
                    if j >= LAG or not first:
                        take_transposed(TILES * i + j - LAG, (j - LAG) % TILES)
                    if first and j == 2:
                        k_high(1)
                    if last and j == 0:
                        act.wait_ge(ld_small, 16 * 7)
                        act.activation(mask_t[:], bits[:, 2, :], ACT.Tanh, scale=0.5).then_inc(mask_made, 1)
                    if last and 1 <= j <= 4:
                        if j == 1:
                            act.wait_ge(ld_ffn, 32)
                        w, ot = (pw, nw)[(j - 1) % 2], (j - 1) // 2
                        act.activation(w[:, ot, :], w[:, ot, :], ACT.Tanh, scale=0.5).then_inc(tanh_made, 1)

            take_step(CT_)
            take_step(C_)
            take_hq(0)
            take_step(V_)
            k_high(0)
            take_step(MT_)
            take_step(M_)
            q_high(q_count(0, 0), 0, work[Q0 % 2])
            take_hq(1)
            one_pair(0, first=True)
            with act.Fori(1, NP - 1) as i:
                one_pair(i)
            one_pair(NP - 1, last=True)
            take_transposed(TILES * NP - 3, TILES - 3)
            act.wait_ge(ffn_w_transposed, 1)
            act.activation(w_ffn_t[:].rearrange("p t d -> p (t d)"), score_bank[0][:], ACT.Copy)\
               .then_inc(ffn_w_taken, 1)
            for j in (TILES - 2, TILES - 1):
                take_transposed(TILES * (NP - 1) + j, j)
            for t in range(T):
                act.wait_ge(h_transposed, t + 1)
                act.activation(h_t[:, t % 2, :], trans_bank[t % 2][:, 0:D], ACT.Copy).then_inc(h_taken, 1)

        @block.vector
        def _(dve):
            chain = [0]

            def link(instruction):
                chain[0] += 1
                instruction.then_inc(dve_chain, 1)
                dve.wait_ge(dve_chain, chain[0])

            def norm_stats(rows, t):
                link(dve.bn_stats(stats[:, t, :], rows[:, t, :]))
                link(dve.bn_aggr(moments[:, t, :], stats[:, t, :]))

            def norm_apply(rows, t, count):
                dve.wait_ge(rstd_made, count)
                dve.tensor_scalar(xn[:, t, :], rows[:, t, :], moments[:, t, 0:1], rstd[:, t:t + 1],
                                  ALU.subtract, ALU.mult).then_inc(xn_made, 1)

            def turn_wk(p):
                dve.wait_ge(ld_wk, 16 * (QH // BK) * (p + 1))
                dve.transpose(wk_t[:], wk[:]).then_inc(wk_turned, 1)

            def turn_wo(p):
                dve.wait_ge(ld_wo, 16 * 2 * (K // BK) * (p + 1))
                dve.transpose(wo_t[:], wo[:]).then_inc(wo_turned, 1)

            def first_stats(b):
                dve.wait_ge(ld_x[b], 16)
                for t in range(b * TT, b * TT + TT):
                    norm_stats(x_rows, t)
                dve.tensor_scalar(var_eps[:, b * TT:b * TT + TT], moments[:, b * TT:b * TT + TT, 1], EPS, None,
                                  ALU.add).then_inc(var_made, 1)

            def k_low(b):
                dve.wait_ge(k_hi_made, b + 1)
                dve.tensor_tensor(k_lo[:, b, :], trans_bank[b][:], k_hi[:, b, :].bitcast(f32),
                                  ALU.subtract).then_inc(k_taken, 1)

            first_stats(0)
            turn_wk(0)
            for t in range(TT):
                norm_apply(x_rows, t, 1)
            dve.wait_ge(ld_rope, 16)
            rope(dve, 0, dve_chain, chain)
            first_stats(1)
            for t in range(TT, T):
                norm_apply(x_rows, t, 2)
            k_low(0)
            turn_wo(0)

            def take_step(i, n):
                dve.wait_ge(work_made, step_count(i, n))
                to, what = step_target(i, n)
                dve.tensor_copy(to, what).then_inc(work_taken, 1)

            def q_low(p, b, g):
                dve.wait_ge(q_hi_made, 2 * p + b + 1)
                for h in range(2):
                    last = dve.tensor_tensor(q_hl[64:128, 2 * b + h, :], g[64 * h:64 * h + 64, 0:S],
                                             q_hl[0:64, 2 * b + h, :].bitcast(f32), ALU.subtract)
                last.then_inc(work_taken, 1)

            def maxima(t, j):
                dve.wait_ge(scored, t + 1)
                dve.tensor_reduce(neg_max[:, j:j + 1], score_bank[j % 2][:], axis=AX, op=ALU.max,
                                  negate=True).then_inc(max_made, 1)

            def inverses(t, j):
                dve.wait_ge(exp_made, t + 1)
                dve.reciprocal(row_inv[:, j:j + 1], row_sum[:, j:j + 1]).then_inc(inv_made, 1)

            def take_ctx(i, b):
                dve.wait_ge(ctx_made, B * i + b + 1)
                dve.tensor_copy(ctx_t[:, bass.ds(i, 1), b * S:b * S + S].rearrange("q a s -> q (a s)"),
                                ctx_bank[:, 0:S]).then_inc(ctx_taken, 1)

            def ffn_weights(j):
                if j == 0:
                    dve.wait_ge(mask_made, 1)
                    link(dve.tensor_scalar(bits[:, 3, :], mask_t[:], 0.5, 0.5, ALU.mult, ALU.add))
                    link(dve.tensor_tensor(bits[:, 3, :], bits[:, 3, :], bits[:, 0, :], ALU.mult))
                    link(dve.tensor_scalar(bits[:, 3, :], bits[:, 3, :], scales[:, 0:1], 0.5, ALU.mult, ALU.mult))
                if j == 1:
                    link(dve.tensor_tensor(pb[:], pb[:], nb[:], ALU.subtract))
                    for t in range(DT):
                        last = dve.tensor_tensor(pb[:, t, :], pb[:, t, :], bits[:, 1, :], ALU.mult)
                    link(last)
                    link(dve.tensor_reduce(b_raw[:], pb[:], axis=AX, op=ALU.add))
                    link(dve.tensor_scalar(b_raw[:], b_raw[:], -1.0, 1.0, ALU.max, ALU.min))
                    link(dve.tensor_scalar(b_raw[:], b_raw[:], LEVELS, ROUND, ALU.mult, ALU.add))
                    link(dve.tensor_scalar(b_raw[:], b_raw[:], -ROUND, 1.0 / LEVELS, ALU.add, ALU.mult))
                    dve.tensor_scalar(b_col[:], b_raw[:], scales[:, 1:2], None, ALU.mult).then_inc(bias_made, 1)
                if j in (3, 5):
                    ot = (j - 3) // 2
                    dve.wait_ge(tanh_made, 2 * ot + 2)
                    link(dve.tensor_tensor(pw[:, ot, :], pw[:, ot, :], nw[:, ot, :], ALU.subtract))
                if j in (4, 6):
                    ot = (j - 4) // 2
                    w_bits = pw[:, ot, :].rearrange("o (i n) -> o i n", n=NB)
                    link(dve.tensor_scalar(w_ffn[:, ot, :], w_bits[:, :, 0], bits[:, 3, 0:1], None, ALU.mult))
                    for n in range(1, NB):
                        last = dve.scalar_tensor_tensor(w_ffn[:, ot, :], w_bits[:, :, n], bits[:, 3, n:n + 1],
                                                        w_ffn[:, ot, :], ALU.mult, ALU.add)
                        if n < NB - 1:
                            link(last)
                    last.then_inc(ffn_w_made, 1)

            def one_pair(i, first=False, last=False):
                for j in range(TILES):
                    maxima(TILES * i + j, j)
                    if j >= 1 or not first:
                        inverses(TILES * i + j - 1, (j - 1) % TILES)
                    if first and j == 2:
                        k_low(1)
                    if j == 0 and not last:
                        turn_wk(i + 1)
                    if j == SLOT_OF[N_]:
                        take_step(i, N_)
                    if j == slot_of(Q1, last):
                        q_low(i, 1, work[Q1 % 2])
                    if not last:
                        if j == 5:
                            turn_wo(i + 1)
                        for n in range(CT_, Q0):
                            if SLOT_OF[n] == j:
                                take_step(i, n)
                        if j == SLOT_OF[Q0]:
                            q_low(i + 1, 0, work[Q0 % 2])
                    if j == LAG and not first:
                        take_ctx(i - 1, 1)
                    if j == 4 + LAG:
                        take_ctx(i, 0)
                    if last:
                        ffn_weights(j)

            q_low(0, 0, work[Q0 % 2])
            one_pair(0, first=True)
            with dve.Fori(1, NP - 1) as i:
                one_pair(i)
            one_pair(NP - 1, last=True)
            inverses(TILES * NP - 1, TILES - 1)
            def residual(t):
                dve.wait_ge(attn_out, TT * (t // TT + 1))
                dve.tensor_tensor(x2[:, t, :], projected(t), x_rows[:, t, :], ALU.add)\
                   .then_inc(x2_made, 1)
                dve.wait_ge(x2_made, t + 1)
                norm_stats(x2, t)
                dve.tensor_scalar(var_eps[:, t:t + 1], moments[:, t, 1:2], EPS, None, ALU.add)\
                   .then_inc(var_made, 1)
                norm_apply(x2, t, B + t + 1)

            def finish(t):
                dve.wait_ge(ffn_out, t + 1)
                dve.wait_ge(x2b_made, t + 1)
                dve.tensor_tensor(y[:, t, :], score_bank[t % 2][:, 0:D], x2b[:, t, :], ALU.add).then_inc(y_made, 1)

            residual(0)
            residual(1)
            dve.wait_ge(bias_spread, 1)
            dve.tensor_copy(b_rows[:], score_bank[1][:, 0:D]).then_inc(bias_taken, 1)
            take_ctx(NP - 1, 1)
            finish(0)
            residual(2)
            residual(3)
            for t in range(1, T):
                finish(t)

        @block.tensor
        def _(pe):
            pe.wait_ge(ident_made, 1)
            def transpose_keys(b):
                pe.wait_ge(kv_made[b], 1)
                for lt in range(LT):
                    last = pe.transpose(trans_bank[b][:, lt * P:lt * P + P], kv[:, b * LT + lt, :], ident[:])
                last.then_inc(k_transposed, 1)

            def transpose_input(b):
                pe.wait_ge(xn_made, TT * (b + 1))
                for n in range(DT):
                    for t in range(TT):
                        last = pe.transpose(score_bank[b][:, n * S + t * P:n * S + t * P + P],
                                            xn[:, b * TT + t, n * P:n * P + P], ident[:])
                last.then_inc(hq_transposed, 1)

            def prepare(i, n, free=False):
                g = work[n % 2]
                p = i if n == N_ else i + 1
                if n in (C_, V_, MT_, M_):
                    pe.wait_ge(work_taken, step_count(i, n) - 1)
                elif not free:
                    pe.wait_ge(work_taken, step_count(i, n) - 2)
                if n == CT_:
                    pe.wait_ge(ld_wkr, 32 * (p + 1))
                    pe.transpose(g[:, 0:P], wkr[:], ident[:])
                    pe.wait_ge(ld_wqr, 16 * (p + 1))
                    pe.wait_ge(wk_turned, p + 1)
                    for s in range(2):
                        for h in range(2):
                            last = pe.matmul(g[64 * h:64 * h + 64, P:P + K], wqr[:, 2 * h + s, :],
                                             wk_t[:, s, h * K:h * K + K], start=(s == 0), stop=(s == 1))
                elif n == N_:
                    pe.wait_ge(ld_wkv, 16 * (p + 1))
                    pe.wait_ge(wo_turned, p + 1)
                    for h in range(2):
                        last = pe.matmul(g[64 * h:64 * h + 64, 0:D], wkv[:, h, :], wo_t[:, h, :],
                                         start=True, stop=True)
                elif n == C_:
                    last = pe.transpose(g[:, 0:P], wkr_c[:, P:2 * P], ident[:])
                elif n == V_:
                    pe.wait_ge(ld_wq, 16 * (p + 1))
                    for h in range(2):
                        last = pe.matmul(g[64 * h:64 * h + 64, 0:D], c[:, h * R:h * R + R], wq[:, h, :],
                                         start=True, stop=True)
                elif n == MT_:
                    last = pe.matmul(g[:, 0:D], wkr_c[:, 0:P], v[:], start=True, stop=True)
                elif n == M_:
                    for t in range(DT):
                        last = pe.transpose(g[:, t * P:t * P + P], m_t[:, t * P:t * P + P], ident[:])
                last.then_inc(work_made, 1)

            def queries(p, b, n):
                pe.wait_ge(work_taken, q_count(p, b) - (2 if b else 1))
                for t in range(DT):
                    last = pe.matmul(work[n % 2][:, 0:S], m[:, t, :], hq_t[:, b, t, :],
                                     start=(t == 0), stop=(t == DT - 1))
                last.then_inc(work_made, 1)

            def scores(i, t, j):
                b, h, tt = j // (2 * TT), j // TT % 2, j % TT
                if j % (2 * TT) == 0:
                    pe.wait_ge(work_taken, q_count(i, b))
                pe.wait_ge(exp_made, t - 1)
                q = q_hl[:, 2 * b + h, tt * P:tt * P + P]
                pe.matmul(score_bank[j % 2][:], q, k_hi[:, b, :], start=True, stop=False)
                pe.matmul(score_bank[j % 2][:], q, k_lo[:, b, :], start=False, stop=True).then_inc(scored, 1)

            def transpose_probs(t, j, fresh=False):
                pe.wait_ge(norm_made, t + 1)
                if not fresh:
                    pe.wait_ge(probs_taken, t - 1)
                for lt in range(LT):
                    last = pe.transpose(trans_bank[j % 2][:, lt * P:lt * P + P],
                                        probs[:, j, lt * P:lt * P + P], ident[:])
                last.then_inc(transposed, 1)

            def contexts(i, b, fresh=False):
                pe.wait_ge(probs_taken, TILES * i + 2 * TT * (b + 1))
                if not fresh:
                    pe.wait_ge(ctx_taken, B * i + b)
                for lt in range(LT):
                    for h in range(2):
                        last = pe.matmul(ctx_bank[64 * h:64 * h + 64, 0:S],
                                         kv[:, b * LT + lt, h * DC:h * DC + DC], probs_t[:, b, lt, h, :],
                                         start=(lt == 0), stop=(lt == LT - 1))
                last.then_inc(ctx_made, 1)

            def one_pair(i, first=False, last=False):
                for j in range(TILES):
                    t = TILES * i + j
                    if first and j in (0, 2 * TT):
                        pe.wait_ge(k_taken, j // (2 * TT) + 1)
                    if first and j < 2:
                        scores_first(j)
                    else:
                        scores(i, t, j)
                    if j == SLOT_OF[N_]:
                        prepare(i, N_)
                    if j == slot_of(Q1, last):
                        queries(i, 1, Q1)
                    if first and j == 2:
                        transpose_keys(1)
                    if not last:
                        for n in range(CT_, Q0):
                            if SLOT_OF[n] == j:
                                prepare(i, n)
                    if j >= LAG or not first:
                        transpose_probs(t - LAG, (j - LAG) % TILES, fresh=first and j < LAG + 2)
                    if not last and j == SLOT_OF[Q0]:
                        queries(i + 1, 0, Q0)
                    if last and j >= 1:
                        if j == 1:
                            pe.wait_ge(work_taken, q_count(i, 1))
                        for t_q in range(T):
                            project(t_q, j - 1)
                    if j == LAG and not first:
                        contexts(i - 1, 1)
                    if j == 4 + LAG:
                        contexts(i, 0, fresh=first)

            def scores_first(j):
                pe.wait_ge(hq_taken, j + 1)
                if j == 0:
                    pe.wait_ge(work_taken, q_count(0, 0))
                q = q_hl[:, 0, j * P:j * P + P]
                pe.matmul(score_bank[j][:], q, k_hi[:, 0, :], start=True, stop=False)
                pe.matmul(score_bank[j][:], q, k_lo[:, 0, :], start=False, stop=True).then_inc(scored, 1)

            def project(t, p):
                last = pe.matmul(projected(t), ctx_t[:, p, t * P:t * P + P], n_all[:, p, :],
                                 start=(p == 0 and t % TT == 0), stop=(p == NP - 1), skip_group_check=True)
                if p == NP - 1:
                    last.then_inc(attn_out, 1)

            prepare(-1, CT_, free=True)
            prepare(-1, C_)
            transpose_input(0)
            prepare(-1, V_)
            transpose_keys(0)
            prepare(-1, MT_)
            prepare(-1, M_)
            transpose_input(1)
            pe.wait_ge(hq_taken, 1)
            queries(0, 0, Q0)
            one_pair(0, first=True)
            with pe.Fori(1, NP - 1) as i:
                one_pair(i)
            one_pair(NP - 1, last=True)

            def transpose_hidden(t):
                pe.wait_ge(xn_made, T + t + 1)
                if t >= 2:
                    pe.wait_ge(h_taken, t - 1)
                for n in range(DT):
                    last = pe.transpose(trans_bank[t % 2][:, n * P:n * P + P], xn[:, t, n * P:n * P + P], ident[:])
                last.then_inc(h_transposed, 1)

            def ffn(t):
                pe.wait_ge(h_taken, t + 1)
                if t >= 2:
                    pe.wait_ge(y_made, t - 1)
                for n in range(DT):
                    last = pe.matmul(score_bank[t % 2][:, 0:D], h_t[:, t % 2, n * P:n * P + P], w_ffn_t[:, n, :],
                                     start=(n == 0), stop=(n == DT - 1))
                last.then_inc(ffn_out, 1)

            transpose_probs(TILES * NP - 3, TILES - 3)
            pe.wait_ge(ctx_taken, B * NP - 1)
            for t in range(TT):
                project(t, NP - 1)
            pe.wait_ge(ffn_w_made, DT)
            pe.wait_ge(exp_made, TILES * NP)
            for it in range(DT):
                for ot in range(DT):
                    last = pe.transpose(score_bank[0][:, it * D + ot * P:it * D + ot * P + P],
                                        w_ffn[:, ot, it * P:it * P + P], ident[:])
            last.then_inc(ffn_w_transposed, 1)
            transpose_probs(TILES * NP - 2, TILES - 2)
            pe.wait_ge(bias_made, 1)
            for ot in range(DT):
                last = pe.matmul(score_bank[1][:, ot * P:ot * P + P], b_col[:, ot:ot + 1].broadcast_to([P, P]),
                                 ident[:], start=True, stop=True)
            last.then_inc(bias_spread, 1)
            transpose_probs(TILES * NP - 1, TILES - 1)
            contexts(NP - 1, 1)
            for t in range(TT):
                transpose_hidden(t)
            pe.wait_ge(ffn_w_taken, 1)
            ffn(0)
            pe.wait_ge(ctx_taken, B * NP)
            for t in range(TT, T):
                project(t, NP - 1)
            pe.wait_ge(bias_taken, 1)
            ffn(1)
            for t in range(TT, T):
                transpose_hidden(t)
                ffn(t)


_INS = ["x", "ctx_512", "L0_xattn_Wq", "L0_xattn_w_kc_q", "L0_xattn_w_kc_kv", "L0_xattn_W_qr", "L0_xattn_W_kr",
        "L0_xattn_Wo", "L0_ffn_pweight", "L0_ffn_nweight", "L0_ffn_exps", "L0_ffn_bexps", "L0_ffn_mask_weight",
        "L0_ffn_scale", "L0_ffn_pbias", "L0_ffn_nbias", "L0_ffn_biasscale"]


def rope_table():
    f = np.float32
    inv_freq = f(1.0) / np.power(10000.0, np.arange(0, DC, 2) / DC).astype(f)
    angle = np.arange(L, dtype=f)[:, None] * inv_freq[None, :]
    sin = np.repeat(np.sin(angle), 2, axis=-1)
    cos = np.repeat(np.cos(angle), 2, axis=-1)
    sin[:, :DC // 2] = -sin[:, :DC // 2]
    return np.concatenate([cos, sin], axis=-1).astype(f)


def kernel(**inputs):
    import concourse.bacc as _bacc
    from concourse.bass_utils import run_bass_kernel_spmd as _run

    nc = _bacc.Bacc("TRN2", target_bir_lowering=False, num_devices=1)
    given = [(name, np.ascontiguousarray(inputs[name])) for name in _INS] + [("rope_table", rope_table())]
    arrays, args = {}, []
    for name, a in given:
        arrays[f"in_{name}_dram"] = a
        args.append(nc.dram_tensor(f"in_{name}_dram", a.shape, mybir.dt.from_np(a.dtype), kind="ExternalInput").ap())
    args.append(nc.dram_tensor("out_0_dram", (B, S, D), mybir.dt.float32, kind="ExternalOutput").ap())
    xattn_ffn_kernel(nc, *args)
    r = _run(nc, [arrays], core_ids=[0])
    return r.results[0]["out_0_dram"]
```

```python
from contextlib import ExitStack

import concourse.bass as bass
from concourse import mybir
from concourse.alu_op_type import AluOpType as ALU

import numpy as np

B, S, D = 2, 256, 256
L, DC = 512, 64
H, K, CQ, R = 16, 128, 192, 64
NB = 4
P = 128
TT = S // P
T = B * TT
LT = L // P
DT = D // P
NP = H // 2
QH = CQ // 2
BK = 32
TILES = B * 2 * TT
LAG = 3
IDLE_PRODUCTS = 10
EPS = 1e-5
LEVELS = float(2 ** NB - 1)
ROUND = 1.5 * 2.0 ** 23

N_, Q1, CT_, E_, MT_, M_, Q0 = range(7)
STEPS = 7
SLOT_OF = {N_: 0, Q1: 1, CT_: 2, E_: 3, MT_: 4, M_: 5, Q0: 6}
BANK_OF = {N_: 0, Q1: 1, CT_: 0, E_: 1, MT_: 0, M_: 1, Q0: 2}


def step_count(i, n):
    return STEPS * (i + 1) + n + 1 - CT_


def q_count(p, b):
    return step_count(p, Q1) if b else step_count(p - 1, Q0)


EARLIER_PRODUCTS = ([(t, p) for p in range(2) for t in (0, 1, 3)] + [(2, 0), (2, 1)]
                    + [(t, p) for p in range(2, NP - 1) for t in range(T)])


def tile_of(j):
    return j // (2 * TT), j % 2, j // 2 % TT


def xattn_ffn_kernel(nc, x, ctx_512, Wq, w_kc_q, w_kc_kv, W_qr, W_kr, Wo, pweight, nweight, exps, bexps,
                     mask_weight, scale, pbias, nbias, biasscale, rope_table, out):
    f32 = mybir.dt.float32
    f32r = mybir.dt.float32r
    ACT = mybir.ActivationFunctionType
    AX = mybir.AxisListType.X

    x_dram = x.rearrange("b (t p) d -> p (b t) d", p=P)
    out_dram = out.rearrange("b (t p) d -> p (b t) d", p=P)
    ctx_dram = ctx_512.rearrange("b (p t) d -> p b t d", p=P)
    rope_dram = rope_table.rearrange("(p t) d -> p t d", p=P)
    wq_dram = Wq.rearrange("(h k) d -> k h d", k=K)
    wk_dram = w_kc_q.rearrange("h (i r) (s j c) -> j r s (h i) c", r=BK, s=2, c=BK)
    wkv_dram = w_kc_kv.rearrange("h k d -> k h d")
    wqr_dram = W_qr.rearrange("h (s q) r -> q (h s) r", s=2)
    wkr_dram = W_kr.rearrange("h (b v) (a u) -> a v h b u", v=BK, u=BK)
    wo_dram = Wo.rearrange("(i r) (h j c) -> j r h i c", r=BK, j=K // BK, c=BK)
    pw_dram = pweight.rearrange("(t o) i n -> o t (i n)", o=P)
    nw_dram = nweight.rearrange("(t o) i n -> o t (i n)", o=P)
    pb_dram = pbias.rearrange("(t o) n -> o t n", o=P)
    nb_dram = nbias.rearrange("(t o) n -> o t n", o=P)

    with ExitStack() as stack:
        def sb(name, shape, dt=f32):
            return stack.enter_context(nc.sbuf_tensor(name, shape, dt))

        def bank(name):
            return stack.enter_context(nc.psum_tensor(name, [P, 512], f32))

        def sem(name):
            return stack.enter_context(nc.semaphore(name))

        x_rows = sb("x_rows", [P, T, D])
        ctx_rows = sb("ctx_rows", [P, B * LT, DC])
        cos_sin = sb("cos_sin", [P, LT, 2 * DC])
        wq = sb("wq", [P, 2, D])
        wk_wkr = sb("wk_wkr", [P, 4 * K + P])
        wk = wk_wkr[0:QH, 0:4 * K].rearrange("q (s k) -> q s k", s=2)
        wkr = wk_wkr[:, 4 * K:4 * K + P]
        wkv = sb("wkv", [P, 2, DC])
        wqr = sb("wqr", [QH, 4, R])
        wo = sb("wo", [P, 2, D])
        pw = sb("pw", [P, DT, D * NB])
        nw = sb("nw", [P, DT, D * NB])
        pb = sb("pb", [P, DT, NB])
        nb = sb("nb", [P, DT, NB])
        bits = sb("bits", [P, 4, NB])
        mask_t = sb("mask_t", [P, NB])
        scales = sb("scales", [P, 2])
        ident = sb("ident", [P, P])
        warm = sb("warm", [P, 1])
        idle = sb("idle", [P, P])
        neg_half = sb("neg_half", [P, T])
        stats = sb("stats", [P, T, 6])
        moments = sb("moments", [P, T, 2])
        var_eps = sb("var_eps", [P, T])
        rstd = sb("rstd", [P, T])
        xn = sb("xn", [P, T, D])
        hq_t = sb("hq_t", [P, B, DT, S])
        rot = sb("rot", [P, B * LT, DC])
        kv = sb("kv", [P, B * LT, 2 * DC])
        k_hi = sb("k_hi", [P, B, L], f32r)
        k_lo = sb("k_lo", [P, B, L], f32r)
        wk_wkr_t = sb("wk_wkr_t", [P, 4 * K + P])
        wk_t = wk_wkr_t[0:QH, 0:4 * K].rearrange("q (s k) -> q s k", s=2)
        wkr_t = wk_wkr_t[:, 4 * K:4 * K + P]
        wo_t = sb("wo_t", [P, 2, D])
        c_t = sb("c_t", [P, K])
        e = sb("e", [P, 2 * DC])
        m_t = sb("m_t", [P, D])
        m = sb("m", [P, DT, 2 * DC])
        q_hl = sb("q_hl", [P, 2 * B, S], f32r)
        n_all = sb("n_all", [P, NP, D])
        neg_max = sb("neg_max", [P, TILES])
        row_sum = sb("row_sum", [P, TILES])
        row_inv = sb("row_inv", [P, TILES])
        probs = sb("probs", [P, TILES, L])
        probs_t = sb("probs_t", [P, B, LT, 2, S])
        ctx_t = sb("ctx_t", [P, NP, T * P])
        w_ffn = sb("w_ffn", [P, DT, D])
        w_ffn_t = sb("w_ffn_t", [P, DT, D])
        b_raw = sb("b_raw", [P, DT])
        b_col = sb("b_col", [P, DT])
        b_rows = sb("b_rows", [P, D])
        x2 = sb("x2", [P, T, D])
        x2b = sb("x2b", [P, T, D])
        h_t = sb("h_t", [P, T, D])
        y = sb("y", [P, T, D])

        score_bank = [bank("score0"), bank("score1")]
        trans_bank = [bank("trans0"), bank("trans1")]
        ctx_bank = bank("ctxb")
        work = [bank("work0"), bank("work1"), bank("work2")]
        input_bank = [score_bank[0], ctx_bank]
        ffn_bank = score_bank + work[:2]

        ld_rope, ld_small, ld_ffn = (sem("ld_" + s) for s in ("rope", "small", "ffn"))
        ld_x, ld_ctx = ([sem(f"ld_{s}{b}") for b in range(B)] for s in ("x", "ctx"))
        ld_wq, ld_wk, ld_wkv, ld_wqr, ld_wkr, ld_wo = (
            sem("ld_" + s) for s in ("wq", "wk", "wkv", "wqr", "wkr", "wo"))
        ld_first_wqr = sem("ld_first_wqr")
        ident_made = sem("ident_made")
        zeros_made = sem("zeros_made")
        margin_made = sem("margin_made")
        idle_made = sem("idle_made")
        neg_half_made = sem("neg_half_made")
        rstd_made = sem("rstd_made")
        dve_chain = sem("dve_chain")
        pool_chain = sem("pool_chain")
        act_chain = sem("act_chain")
        mask_made = sem("mask_made")
        var_made = sem("var_made")
        xn_made = sem("xn_made")
        wk_turned = sem("wk_turned")
        first_wkr_transposed = sem("first_wkr_transposed")
        first_wkr_taken = sem("first_wkr_taken")
        wo_turned = sem("wo_turned")
        hq_transposed = sem("hq_transposed")
        hq_taken = sem("hq_taken")
        kv_made = [sem(f"kv_made{b}") for b in range(B)]
        k_transposed = sem("k_transposed")
        k_hi_made = sem("k_hi_made")
        k_taken = sem("k_taken")
        work_made = sem("work_made")
        work_taken = sem("work_taken")
        q_hi_made = sem("q_hi_made")
        scored = sem("scored")
        max_made = sem("max_made")
        exp_made = sem("exp_made")
        inv_made = sem("inv_made")
        inv_seen = sem("inv_seen")
        norm_made = sem("norm_made")
        transposed = sem("transposed")
        probs_taken = sem("probs_taken")
        ctx_made = sem("ctx_made")
        ctx_taken = sem("ctx_taken")
        tanh_made = sem("tanh_made")
        ffn_w_made = sem("ffn_w_made")
        bias_made = sem("bias_made")
        ffn_w_transposed = sem("ffn_w_transposed")
        ffn_w_taken = sem("ffn_w_taken")
        bias_spread = sem("bias_spread")
        bias_taken = sem("bias_taken")
        attn_out = sem("attn_out")
        x2_made = sem("x2_made")
        h_transposed = sem("h_transposed")
        h_taken = sem("h_taken")
        ffn_out = sem("ffn_out")
        x2b_made = sem("x2b_made")
        y_made = sem("y_made")
        stored = sem("stored")

        block = stack.enter_context(nc.Block())

        def load_wk(eng, p, j):
            eng.dma_start(wk[j * BK:j * BK + BK, :, :].rearrange("r s (i c) -> r s i c", c=BK),
                          wk_dram[j, :, :, bass.ds(8 * p, 8), :]).then_inc(ld_wk, 16)

        @block.sync
        def _(sp):
            def pair_of(dram, p):
                return dram[:, bass.ds(2 * p, 2), :]

            def load_queries_side(p):
                sp.wait_ge(wk_turned, p)
                sp.wait_ge(first_wkr_transposed, 1)
                for j in range(QH // BK):
                    load_wk(sp, p, j)
                for h in range(2):
                    for a in range(R // BK):
                        rows = 64 * h + BK * a
                        sp.dma_start(wkr[rows:rows + BK, 64 * h:64 * h + 64].rearrange("v (b u) -> v b u", u=BK),
                                     wkr_dram[a, :, bass.ds(2 * p + h, 1), :, :].rearrange("v h b u -> v (h b) u"))\
                          .then_inc(ld_wkr, 16)
                sp.wait_ge(work_made, step_count(p - 2, CT_))
                sp.dma_start(wqr[:], wqr_dram[:, bass.ds(4 * p, 4), :]).then_inc(ld_wqr, 16)
                sp.wait_ge(work_made, step_count(p - 2, MT_))
                sp.dma_start(wq[:], pair_of(wq_dram, p)).then_inc(ld_wq, 16)

            def load_values_side(p, first=False):
                if not first:
                    sp.wait_ge(wo_turned, p)
                for j in range(K // BK):
                    for h in range(2):
                        sp.dma_start(wo[j * BK:j * BK + BK, h, :].rearrange("r (i c) -> r i c", c=BK),
                                     wo_dram[j, :, bass.ds(2 * p + h, 1), :, :].rearrange("r h i c -> r (h i) c"))\
                          .then_inc(ld_wo, 16)
                if not first:
                    sp.wait_ge(work_made, step_count(p - 1, N_))
                sp.dma_start(wkv[:], pair_of(wkv_dram, p)).then_inc(ld_wkv, 16)

            load_wk(sp, 0, 0)
            load_wk(sp, 0, 2)
            sp.wait_ge(zeros_made, 1)
            for h in range(2):
                sp.dma_start(wkr[64 * h:64 * h + 64, 64 * h:64 * h + 64], W_kr[h, :, :]).then_inc(ld_wkr, 16)
            sp.dma_start(ctx_rows[:, 0:LT, :], ctx_dram[:, 0, :, :]).then_inc(ld_ctx[0], 16)
            sp.dma_start(wq[:], pair_of(wq_dram, 0)).then_inc(ld_wq, 16)
            load_values_side(0, first=True)
            with sp.Fori(1, NP) as p:
                load_queries_side(p)
                load_values_side(p)
            for n, vec in enumerate((exps, bexps, mask_weight)):
                sp.dma_start(bits[:, n, :], vec.rearrange("(a n) -> a n", a=1).broadcast_to([P, NB]))\
                  .then_inc(ld_small, 16)
            for n, vec in enumerate((scale, biasscale)):
                sp.dma_start(scales[:, n:n + 1], vec.rearrange("(a n) -> a n", a=1).broadcast_to([P, 1]))\
                  .then_inc(ld_small, 16)
            sp.dma_start(pb[:], pb_dram).then_inc(ld_small, 16)
            sp.dma_start(nb[:], nb_dram).then_inc(ld_small, 16)
            sp.dma_start(pw[:], pw_dram).then_inc(ld_ffn, 16)
            sp.dma_start(nw[:], nw_dram).then_inc(ld_ffn, 16)
            for t in range(T):
                sp.wait_ge(y_made, t + 1)
                sp.dma_start(out_dram[:, t, :], y[:, t, :]).then_inc(stored, 16)
            sp.wait_ge(stored, 16 * T)

        def projected(t):
            return work[max(t - 1, 0)][:, (t == 1) * D:(t == 1) * D + D]

        def step_target(i, n):
            g = work[BANK_OF[n]]
            if n == N_:
                return n_all[:, bass.ds(i, 1), :].rearrange("q a d -> q (a d)"), g[:, 0:D]
            return {
                CT_: (c_t[:], g[:, 0:K]),
                E_: (e[:], g[:, 0:2 * DC]),
                MT_: (m_t[:], g[:, 0:D]),
                M_: (m[:].rearrange("q t d -> q (t d)"), g[:, 0:D]),
            }[n]

        def rope(eng, b, sem_of, count):
            half = DC // 2
            rows = slice(b * LT, b * LT + LT)

            def chained(instruction):
                count[0] += 1
                instruction.then_inc(sem_of, 1)
                eng.wait_ge(sem_of, count[0])

            eng.wait_ge(ld_ctx[b], 16)
            eng.tensor_tensor(rot[:, rows, 0:half], ctx_rows[:, rows, half:DC], cos_sin[:, :, DC:DC + half], ALU.mult)
            chained(eng.tensor_tensor(rot[:, rows, half:DC], ctx_rows[:, rows, 0:half], cos_sin[:, :, DC + half:2 * DC], ALU.mult))
            chained(eng.tensor_tensor(ctx_rows[:, rows, :], ctx_rows[:, rows, :], cos_sin[:, :, 0:DC], ALU.mult))
            for side in range(2):
                last = eng.tensor_tensor(kv[:, rows, side * DC:side * DC + DC], ctx_rows[:, rows, :],
                                         rot[:, rows, :], ALU.add)
            last.then_inc(kv_made[b], 1)

        @block.gpsimd
        def _(pool):
            chain = [0]

            def link(instruction):
                chain[0] += 1
                instruction.then_inc(pool_chain, 1)
                pool.wait_ge(pool_chain, chain[0])

            pool.dma_start(wqr[:], wqr_dram[:, 0:4, :]).then_inc(ld_first_wqr, 16)
            pool.memset(neg_half[:], -0.5).then_inc(neg_half_made, 1)
            link(pool.memset(ident[:], 0.0))
            pool.affine_select(out=ident[:], in_=ident[:], compare_op=ALU.not_equal, fill=1.0, base=0,
                               pattern=[[-1, P]], channel_multiplier=1).then_inc(ident_made, 1)
            pool.dma_start(cos_sin[:], rope_dram).then_inc(ld_rope, 16)
            pool.dma_start(x_rows[:, TT:T, :], x_dram[:, TT:T, :]).then_inc(ld_x[1], 16)
            pool.dma_start(ctx_rows[:, LT:2 * LT, :], ctx_dram[:, 1, :, :]).then_inc(ld_ctx[1], 16)
            pool.wait_ge(neg_half_made, 1)
            for b in range(B):
                pool.wait_ge(var_made, b + 1)
                pool.tensor_tensor(rstd[:, b * TT:b * TT + TT], var_eps[:, b * TT:b * TT + TT],
                                   neg_half[:, 0:TT], ALU.pow).then_inc(rstd_made, 1)
            pool.wait_ge(ld_rope, 16)
            rope(pool, 1, pool_chain, chain)

            def normalise(t, j):
                pool.wait_ge(inv_made, t + 1)
                pool.sem_inc(inv_seen, 1)
                e = probs[:, j, :]
                pool.tensor_scalar(e, e, row_inv[:, j:j + 1], 1.0, ALU.mult, ALU.mult).then_inc(norm_made, 1)

            with pool.Fori(0, NP) as i:
                for j in range(TILES):
                    normalise(TILES * i + j, j)

            def inverse_deviations(tiles, count):
                pool.wait_ge(var_made, B + count)
                pool.tensor_tensor(rstd[:, tiles], var_eps[:, tiles], neg_half[:, tiles], ALU.pow)\
                    .then_inc(rstd_made, 1)

            def residual_bias(t):
                pool.wait_ge(x2_made, t + 1)
                pool.tensor_tensor(x2b[:, t, :], x2[:, t, :], b_rows[:], ALU.add).then_inc(x2b_made, 1)

            inverse_deviations(slice(0, TT), 1)
            pool.wait_ge(bias_taken, 1)
            residual_bias(0)
            inverse_deviations(slice(2, 3), 2)
            residual_bias(1)
            residual_bias(2)
            inverse_deviations(slice(3, 4), 3)
            residual_bias(3)

        @block.scalar
        def _(act):
            load_wk(act, 0, 1)
            act.dma_start(x_rows[:, 0:TT, :], x_dram[:, 0:TT, :]).then_inc(ld_x[0], 16)
            act.wait_ge(neg_half_made, 1)
            act.activation(warm[:], neg_half[:, 0:1], ACT.Exp)

            def take_step(n):
                act.wait_ge(work_made, step_count(-1, n))
                to, what = step_target(-1, n)
                act.activation(to, what, ACT.Copy).then_inc(work_taken, 1)

            def take_hq(b):
                act.wait_ge(hq_transposed, b + 1)
                act.activation(hq_t[:, b, :, :].rearrange("p t s -> p (t s)"), input_bank[b][:], ACT.Copy)\
                   .then_inc(hq_taken, 1)

            def k_high(b):
                act.wait_ge(k_transposed, b + 1)
                act.activation(k_hi[:, b, :], trans_bank[b][:], ACT.Copy).then_inc(k_hi_made, 1)

            def q_high(count, b, g):
                act.wait_ge(work_made, count)
                for h in range(2):
                    act.activation(q_hl[0:64, 2 * b + h, :], g[64 * h:64 * h + 64, 0:S], ACT.Copy)\
                       .then_inc(q_hi_made, 1)

            def exponentials(t, j):
                act.wait_ge(max_made, t + 1)
                act.activation(probs[:, j, :], score_bank[j % 2][:], ACT.Exp, bias=neg_max[:, j:j + 1],
                               accum_out=row_sum[:, j:j + 1]).then_inc(exp_made, 1)

            def take_transposed(t, j):
                act.wait_ge(transposed, t + 1)
                b, h, tt = tile_of(j)
                act.activation(probs_t[:, b, :, h, tt * P:tt * P + P],
                               trans_bank[j % 2][:].rearrange("p (l t) -> p l t", l=LT),
                               ACT.Copy).then_inc(probs_taken, 1)

            def one_pair(i, first=False, last=False):
                for j in range(TILES):
                    if first and j == 0:
                        take_hq(1)
                    if first and j == 2:
                        k_high(1)
                    if j == SLOT_OF[Q1]:
                        q_high(q_count(i, 1), 1, work[BANK_OF[Q1]])
                    hurried = j in (LAG - 1, LAG + 3)
                    if not hurried:
                        exponentials(TILES * i + j, j)
                    if j >= LAG or not first:
                        take_transposed(TILES * i + j - LAG, (j - LAG) % TILES)
                    if hurried:
                        exponentials(TILES * i + j, j)
                    if j == SLOT_OF[Q0] and not last:
                        q_high(q_count(i + 1, 0), 0, work[BANK_OF[Q0]])
                    if last and j == 0:
                        act.wait_ge(ld_small, 16 * 7)
                        act.activation(mask_t[:], bits[:, 2, :], ACT.Tanh, scale=0.5).then_inc(mask_made, 1)
                    if last and 1 <= j <= 4:
                        if j == 1:
                            act.wait_ge(ld_ffn, 32)
                        w, ot = (pw, nw)[(j - 1) % 2], (j - 1) // 2
                        act.activation(w[:, ot, :], w[:, ot, :], ACT.Tanh, scale=0.5).then_inc(tanh_made, 1)

            take_step(CT_)
            act.wait_ge(first_wkr_transposed, 1)
            act.activation(wkr_t, trans_bank[1][:, 0:P], ACT.Copy).then_inc(first_wkr_taken, 1)
            take_step(E_)
            take_step(MT_)
            take_hq(0)
            take_step(M_)
            k_high(0)
            q_high(q_count(0, 0), 0, work[BANK_OF[Q0]])
            one_pair(0, first=True)
            with act.Fori(1, NP - 1) as i:
                one_pair(i)
            one_pair(NP - 1, last=True)
            for j in (TILES - 3, TILES - 2, TILES - 1):
                take_transposed(TILES * (NP - 1) + j, j)
            act.wait_ge(bias_spread, 1)
            act.activation(b_rows[:], score_bank[1][:, 0:D], ACT.Copy).then_inc(bias_taken, 1)
            act.wait_ge(ffn_w_transposed, 1)
            act.activation(w_ffn_t[:].rearrange("p t d -> p (t d)"), score_bank[0][:], ACT.Copy)\
               .then_inc(ffn_w_taken, 1)
            for t in range(T):
                act.wait_ge(h_transposed, t + 1)
                act.activation(h_t[:, t, :], trans_bank[t % 2][:, 0:D], ACT.Copy).then_inc(h_taken, 1)

        @block.vector
        def _(dve):
            chain = [0]

            def link(instruction):
                chain[0] += 1
                instruction.then_inc(dve_chain, 1)
                dve.wait_ge(dve_chain, chain[0])

            def norm_stats(rows, t0, t1):
                for t in range(t0, t1):
                    last = dve.bn_stats(stats[:, t, :], rows[:, t, :])
                link(last)
                for t in range(t0, t1):
                    last = dve.bn_aggr(moments[:, t, :], stats[:, t, :])
                link(last)
                dve.tensor_scalar(var_eps[:, t0:t1], moments[:, t0:t1, 1], EPS, None, ALU.add).then_inc(var_made, 1)

            def norm_apply(rows, t, count):
                dve.wait_ge(rstd_made, count)
                dve.tensor_scalar(xn[:, t, :], rows[:, t, :], moments[:, t, 0:1], rstd[:, t:t + 1],
                                  ALU.subtract, ALU.mult).then_inc(xn_made, 1)

            def turn_wk(p):
                dve.wait_ge(ld_wk, 16 * (QH // BK) * (p + 1))
                dve.wait_ge(ld_wkr, 16 * 2 + 16 * 2 * (R // BK) * p)
                dve.transpose(wk_wkr_t[:], wk_wkr[:]).then_inc(wk_turned, 1)

            def turn_wo(p):
                dve.wait_ge(ld_wo, 16 * 2 * (K // BK) * (p + 1))
                dve.transpose(wo_t[:], wo[:]).then_inc(wo_turned, 1)

            def first_stats(b):
                dve.wait_ge(ld_x[b], 16)
                norm_stats(x_rows, b * TT, b * TT + TT)

            def k_low(b):
                dve.wait_ge(k_hi_made, b + 1)
                dve.tensor_tensor(k_lo[:, b, :], trans_bank[b][:], k_hi[:, b, :].bitcast(f32),
                                  ALU.subtract).then_inc(k_taken, 1)

            dve.memset(idle[:], 0.0).then_inc(idle_made, 1)
            dve.memset(wkr, 0.0).then_inc(zeros_made, 1)
            dve.memset(wk_wkr[QH:P, 0:4 * K], 0.0).then_inc(margin_made, 1)
            dve.wait_ge(ld_wk, 16 * (QH // BK))
            dve.transpose(wk_t, wk).then_inc(wk_turned, 1)
            first_stats(0)
            for t in range(TT):
                norm_apply(x_rows, t, 1)
            dve.wait_ge(margin_made, 1)
            dve.wait_ge(ld_rope, 16)
            rope(dve, 0, dve_chain, chain)
            first_stats(1)
            k_low(0)

            def take_step(i, n):
                dve.wait_ge(work_made, step_count(i, n))
                to, what = step_target(i, n)
                dve.tensor_copy(to, what).then_inc(work_taken, 1)

            def q_low(p, b, g):
                for h in range(2):
                    dve.wait_ge(q_hi_made, 4 * p + 2 * b + h + 1)
                    last = dve.tensor_tensor(q_hl[64:128, 2 * b + h, :], g[64 * h:64 * h + 64, 0:S],
                                             q_hl[0:64, 2 * b + h, :].bitcast(f32), ALU.subtract)
                last.then_inc(work_taken, 1)

            def maxima(t, j):
                dve.wait_ge(scored, t + 1)
                dve.tensor_reduce(neg_max[:, j:j + 1], score_bank[j % 2][:], axis=AX, op=ALU.max,
                                  negate=True).then_inc(max_made, 1)

            def inverses(t, j):
                dve.wait_ge(exp_made, t + 1)
                dve.reciprocal(row_inv[:, j:j + 1], row_sum[:, j:j + 1]).then_inc(inv_made, 1)

            def take_ctx(i, b):
                dve.wait_ge(ctx_made, B * i + b + 1)
                dve.tensor_copy(ctx_t[:, bass.ds(i, 1), b * S:b * S + S].rearrange("q a s -> q (a s)"),
                                ctx_bank[:, 0:S]).then_inc(ctx_taken, 1)

            def ffn_weights(j):
                if j == 0:
                    dve.wait_ge(mask_made, 1)
                    link(dve.tensor_scalar(bits[:, 3, :], mask_t[:], 0.5, 0.5, ALU.mult, ALU.add))
                    link(dve.tensor_tensor(bits[:, 3, :], bits[:, 3, :], bits[:, 0, :], ALU.mult))
                    link(dve.tensor_scalar(bits[:, 3, :], bits[:, 3, :], scales[:, 0:1], 0.5, ALU.mult, ALU.mult))
                if j == 1:
                    link(dve.tensor_tensor(pb[:], pb[:], nb[:], ALU.subtract))
                    for t in range(DT):
                        last = dve.tensor_tensor(pb[:, t, :], pb[:, t, :], bits[:, 1, :], ALU.mult)
                    link(last)
                    link(dve.tensor_reduce(b_raw[:], pb[:], axis=AX, op=ALU.add))
                    link(dve.tensor_scalar(b_raw[:], b_raw[:], -1.0, 1.0, ALU.max, ALU.min))
                    link(dve.tensor_scalar(b_raw[:], b_raw[:], LEVELS, ROUND, ALU.mult, ALU.add))
                    link(dve.tensor_scalar(b_raw[:], b_raw[:], -ROUND, 1.0 / LEVELS, ALU.add, ALU.mult))
                    dve.tensor_scalar(b_col[:], b_raw[:], scales[:, 1:2], None, ALU.mult).then_inc(bias_made, 1)
                if j in (3, 5):
                    ot = (j - 3) // 2
                    dve.wait_ge(tanh_made, 2 * ot + 2)
                    link(dve.tensor_tensor(pw[:, ot, :], pw[:, ot, :], nw[:, ot, :], ALU.subtract))
                if j in (4, 6):
                    ot = (j - 4) // 2
                    w_bits = pw[:, ot, :].rearrange("o (i n) -> o i n", n=NB)
                    link(dve.tensor_scalar(w_ffn[:, ot, :], w_bits[:, :, 0], bits[:, 3, 0:1], None, ALU.mult))
                    for n in range(1, NB):
                        last = dve.scalar_tensor_tensor(w_ffn[:, ot, :], w_bits[:, :, n], bits[:, 3, n:n + 1],
                                                        w_ffn[:, ot, :], ALU.mult, ALU.add)
                        if n < NB - 1:
                            link(last)
                    last.then_inc(ffn_w_made, 1)

            def one_pair(i, first=False, last=False):
                for j in range(TILES):
                    maxima(TILES * i + j, j)
                    if j >= 1 or not first:
                        inverses(TILES * i + j - 1, (j - 1) % TILES)
                    if last and j == TILES - 1:
                        inverses(TILES * i + j, j)
                    if j == 0 and not first:
                        take_ctx(i - 1, 0)
                    if first and j == 0:
                        turn_wo(0)
                    if j == 0 and not first and not last:
                        turn_wk(i + 1)
                    if j == SLOT_OF[N_] + (not last):
                        take_step(i, N_)
                    if first and j == 1:
                        turn_wk(1)
                    if j == SLOT_OF[Q1] + 1:
                        q_low(i, 1, work[BANK_OF[Q1]])
                    if not last:
                        if j == 6:
                            turn_wo(i + 1)
                        for n in range(CT_, Q0):
                            if SLOT_OF[n] == j:
                                take_step(i, n)
                        if j == SLOT_OF[Q0]:
                            q_low(i + 1, 0, work[BANK_OF[Q0]])
                    if first and j == 2:
                        k_low(1)
                    if j == LAG and not first:
                        take_ctx(i - 1, 1)
                    if j == 4 + LAG and last:
                        take_ctx(i, 0)
                    if last:
                        ffn_weights(j)

            q_low(0, 0, work[BANK_OF[Q0]])
            for t in range(TT, T):
                norm_apply(x_rows, t, 2)
            one_pair(0, first=True)
            with dve.Fori(1, NP - 1) as i:
                one_pair(i)
            one_pair(NP - 1, last=True)

            def residual(t):
                dve.wait_ge(attn_out, max(t + 1, TT))
                dve.tensor_tensor(x2[:, t, :], projected(t), x_rows[:, t, :], ALU.add).then_inc(x2_made, 1)

            def take_ctx_tile(tt):
                dve.wait_ge(ctx_made, B * NP + tt)
                dve.tensor_copy(ctx_t[:, NP - 1, S + tt * P:S + tt * P + P], ctx_bank[:, tt * P:tt * P + P])\
                   .then_inc(ctx_taken, 1)

            def finish(t):
                dve.wait_ge(ffn_out, t + 1)
                dve.wait_ge(x2b_made, t + 1)
                dve.tensor_tensor(y[:, t, :], ffn_bank[t][:, 0:D], x2b[:, t, :], ALU.add).then_inc(y_made, 1)

            residual(0)
            residual(1)
            dve.wait_ge(x2_made, 2)
            norm_stats(x2, 0, 2)
            take_ctx_tile(0)
            norm_apply(x2, 0, B + 1)
            norm_apply(x2, 1, B + 1)
            residual(2)
            dve.wait_ge(x2_made, 3)
            norm_stats(x2, 2, 3)
            take_ctx_tile(1)
            norm_apply(x2, 2, B + 2)
            residual(3)
            dve.wait_ge(x2_made, 4)
            norm_stats(x2, 3, 4)
            finish(0)
            norm_apply(x2, 3, B + 3)
            for t in range(1, T):
                finish(t)

        @block.tensor
        def _(pe):
            pe.wait_ge(idle_made, 1)
            for _ in range(IDLE_PRODUCTS):
                pe.matmul(ctx_bank[:, 0:P], idle[:], idle[:], start=True, stop=True)

            pe.wait_ge(ident_made, 1)

            def transpose_keys(b):
                pe.wait_ge(kv_made[b], 1)
                for lt in range(LT):
                    last = pe.transpose(trans_bank[b][:, lt * P:lt * P + P], kv[:, b * LT + lt, :], ident[:])
                last.then_inc(k_transposed, 1)

            def transpose_input(b):
                pe.wait_ge(xn_made, TT * (b + 1))
                for n in range(DT):
                    for t in range(TT):
                        last = pe.transpose(input_bank[b][:, n * S + t * P:n * S + t * P + P],
                                            xn[:, b * TT + t, n * P:n * P + P], ident[:])
                last.then_inc(hq_transposed, 1)

            def prepare(i, n, first=False):
                g = work[BANK_OF[n]]
                p = i if n == N_ else i + 1
                if n in (E_, MT_, M_):
                    pe.wait_ge(work_taken, step_count(i, n) - 1)
                elif not first:
                    pe.wait_ge(work_taken, step_count(i, n) - 2)
                if n == CT_:
                    if first:
                        pe.wait_ge(ld_first_wqr, 16)
                    else:
                        pe.wait_ge(ld_wqr, 16 * p)
                    pe.wait_ge(wk_turned, p + 1)
                    for s in range(2):
                        for h in range(2):
                            last = pe.matmul(g[64 * h:64 * h + 64, 0:K], wqr[:, 2 * h + s, :],
                                             wk_t[:, s, h * K:h * K + K], start=(s == 0), stop=(s == 1))
                elif n == N_:
                    pe.wait_ge(ld_wkv, 16 * (p + 1))
                    pe.wait_ge(wo_turned, p + 1)
                    for h in range(2):
                        last = pe.matmul(g[64 * h:64 * h + 64, 0:D], wkv[:, h, :], wo_t[:, h, :],
                                         start=True, stop=True)
                elif n == E_:
                    pe.wait_ge(wk_turned, p + 1)
                    if first:
                        pe.wait_ge(first_wkr_taken, 1)
                    last = pe.matmul(g[:, 0:2 * DC], c_t[:], wkr_t, start=True, stop=True)
                elif n == MT_:
                    pe.wait_ge(ld_wq, 16 * (p + 1))
                    for h in range(2):
                        last = pe.matmul(g[64 * h:64 * h + 64, 0:D], e[:, h * DC:h * DC + DC], wq[:, h, :],
                                         start=True, stop=True)
                elif n == M_:
                    for t in range(DT):
                        last = pe.transpose(g[:, t * P:t * P + P], m_t[:, t * P:t * P + P], ident[:])
                last.then_inc(work_made, 1)

            def queries(p, b, n):
                pe.wait_ge(work_taken, step_count(p - 1, M_))
                for t in range(DT):
                    last = pe.matmul(work[BANK_OF[n]][:, 0:S], m[:, t, :], hq_t[:, b, t, :],
                                     start=(t == 0), stop=(t == DT - 1))
                last.then_inc(work_made, 1)

            def scores(i, t, j):
                b, h, tt = tile_of(j)
                if j % (2 * TT) == 0:
                    pe.wait_ge(work_taken, q_count(i, b))
                pe.wait_ge(exp_made, t - 1)
                q = q_hl[:, 2 * b + h, tt * P:tt * P + P]
                pe.matmul(score_bank[j % 2][:], q, k_hi[:, b, :], start=True, stop=False)
                pe.matmul(score_bank[j % 2][:], q, k_lo[:, b, :], start=False, stop=True).then_inc(scored, 1)

            def transpose_probs(t, j, fresh=False):
                pe.wait_ge(norm_made, t + 1)
                if not fresh:
                    pe.wait_ge(probs_taken, t - 1)
                for lt in range(LT):
                    last = pe.transpose(trans_bank[j % 2][:, lt * P:lt * P + P],
                                        probs[:, j, lt * P:lt * P + P], ident[:])
                last.then_inc(transposed, 1)

            def contexts(i, b, fresh=False):
                pe.wait_ge(probs_taken, TILES * i + 2 * TT * (b + 1))
                if not fresh:
                    pe.wait_ge(ctx_taken, B * i + b)
                for lt in range(LT):
                    for h in range(2):
                        last = pe.matmul(ctx_bank[64 * h:64 * h + 64, 0:S],
                                         kv[:, b * LT + lt, h * DC:h * DC + DC], probs_t[:, b, lt, h, :],
                                         start=(lt == 0), stop=(lt == LT - 1))
                last.then_inc(ctx_made, 1)

            def one_pair(i, first=False, last=False):
                for j in range(TILES):
                    t = TILES * i + j
                    if first and j in (0, 2 * TT):
                        pe.wait_ge(k_taken, j // (2 * TT) + 1)
                    if first and j < 2:
                        scores_first(j)
                    else:
                        scores(i, t, j)
                    if first and j == 0:
                        transpose_input(1)
                    if j == (1 if first else SLOT_OF[N_]):
                        prepare(i, N_)
                    if j == SLOT_OF[Q1]:
                        if first:
                            pe.wait_ge(hq_taken, 2)
                        queries(i, 1, Q1)
                    if first and j == 2:
                        transpose_keys(1)
                    if not last:
                        for n in (CT_, MT_, M_):
                            if SLOT_OF[n] == j:
                                prepare(i, n)
                    if j >= LAG or not first:
                        transpose_probs(t - LAG, (j - LAG) % TILES, fresh=first and j < LAG + 2)
                    if not last and j == SLOT_OF[E_]:
                        prepare(i, E_)
                    if not last and j == SLOT_OF[Q0]:
                        queries(i + 1, 0, Q0)
                    if last and j >= 2:
                        if j == 2:
                            pe.wait_ge(work_taken, step_count(i, N_))
                        for t_q, p in EARLIER_PRODUCTS[max(5 * j - 12, 0):5 * j - 7]:
                            if t_q == 2 and p == 0:
                                pe.wait_ge(work_taken, q_count(i, 1))
                            project(t_q, p)
                    if j == LAG and not first:
                        contexts(i - 1, 1)
                    if j == 4 + LAG:
                        contexts(i, 0, fresh=first)

            def last_contexts(tt):
                pe.wait_ge(probs_taken, TILES * (NP - 1) + 2 * TT + 2 * (tt + 1))
                pe.wait_ge(ctx_taken, B * NP - 1 + tt)
                for lt in range(LT):
                    for h in range(2):
                        last = pe.matmul(ctx_bank[64 * h:64 * h + 64, tt * P:tt * P + P],
                                         kv[:, LT + lt, h * DC:h * DC + DC], probs_t[:, 1, lt, h, tt * P:tt * P + P],
                                         start=(lt == 0), stop=(lt == LT - 1))
                last.then_inc(ctx_made, 1)

            def scores_first(j):
                if j == 0:
                    pe.wait_ge(work_taken, q_count(0, 0))
                b, h, tt = tile_of(j)
                q = q_hl[:, 2 * b + h, tt * P:tt * P + P]
                pe.matmul(score_bank[j][:], q, k_hi[:, 0, :], start=True, stop=False)
                pe.matmul(score_bank[j][:], q, k_lo[:, 0, :], start=False, stop=True).then_inc(scored, 1)

            def project(t, p):
                last = pe.matmul(projected(t), ctx_t[:, p, t * P:t * P + P], n_all[:, p, :],
                                 start=(p == 0 and t != 1), stop=(p == NP - 1), skip_group_check=True)
                if p == NP - 1:
                    last.then_inc(attn_out, 1)

            prepare(-1, CT_, first=True)
            pe.wait_ge(ld_wkr, 16 * 2)
            pe.transpose(trans_bank[1][:, 0:P], wkr, ident[:]).then_inc(first_wkr_transposed, 1)
            prepare(-1, E_, first=True)
            prepare(-1, MT_)
            transpose_input(0)
            prepare(-1, M_)
            transpose_keys(0)
            pe.wait_ge(hq_taken, 1)
            queries(0, 0, Q0)
            one_pair(0, first=True)
            with pe.Fori(1, NP - 1) as i:
                one_pair(i)
            one_pair(NP - 1, last=True)

            def transpose_hidden(t):
                pe.wait_ge(xn_made, T + t + 1)
                if t >= 2:
                    pe.wait_ge(h_taken, t - 1)
                for n in range(DT):
                    last = pe.transpose(trans_bank[t % 2][:, n * P:n * P + P], xn[:, t, n * P:n * P + P], ident[:])
                last.then_inc(h_transposed, 1)

            def ffn(t):
                pe.wait_ge(h_taken, t + 1)
                for n in range(DT):
                    last = pe.matmul(ffn_bank[t][:, 0:D], h_t[:, t, n * P:n * P + P], w_ffn_t[:, n, :],
                                     start=(n == 0), stop=(n == DT - 1))
                last.then_inc(ffn_out, 1)

            transpose_probs(TILES * NP - 3, TILES - 3)
            pe.wait_ge(ctx_taken, B * NP - 1)
            project(0, NP - 1)
            project(1, NP - 1)
            transpose_probs(TILES * NP - 2, TILES - 2)
            transpose_probs(TILES * NP - 1, TILES - 1)
            last_contexts(0)
            pe.wait_ge(exp_made, TILES * NP)
            pe.wait_ge(bias_made, 1)
            for ot in range(DT):
                last = pe.matmul(score_bank[1][:, ot * P:ot * P + P], b_col[:, ot:ot + 1].broadcast_to([P, P]),
                                 ident[:], start=True, stop=True)
            last.then_inc(bias_spread, 1)
            pe.wait_ge(ctx_taken, B * NP)
            project(2, NP - 1)
            last_contexts(1)
            pe.wait_ge(ffn_w_made, DT)
            for it in range(DT):
                for ot in range(DT):
                    last = pe.transpose(score_bank[0][:, it * D + ot * P:it * D + ot * P + P],
                                        w_ffn[:, ot, it * P:it * P + P], ident[:])
            last.then_inc(ffn_w_transposed, 1)
            for t in range(TT):
                transpose_hidden(t)
            pe.wait_ge(ctx_taken, B * NP + 1)
            project(3, NP - 1)
            pe.wait_ge(ffn_w_taken, 1)
            ffn(0)
            pe.wait_ge(bias_taken, 1)
            ffn(1)
            for t in range(TT, T):
                transpose_hidden(t)
            for t in range(TT, T):
                ffn(t)


_INS = ["x", "ctx_512", "L0_xattn_Wq", "L0_xattn_w_kc_q", "L0_xattn_w_kc_kv", "L0_xattn_W_qr", "L0_xattn_W_kr",
        "L0_xattn_Wo", "L0_ffn_pweight", "L0_ffn_nweight", "L0_ffn_exps", "L0_ffn_bexps", "L0_ffn_mask_weight",
        "L0_ffn_scale", "L0_ffn_pbias", "L0_ffn_nbias", "L0_ffn_biasscale"]


def rope_table():
    f = np.float32
    inv_freq = f(1.0) / np.power(10000.0, np.arange(0, DC, 2) / DC).astype(f)
    angle = np.arange(L, dtype=f)[:, None] * inv_freq[None, :]
    sin = np.repeat(np.sin(angle), 2, axis=-1)
    cos = np.repeat(np.cos(angle), 2, axis=-1)
    sin[:, :DC // 2] = -sin[:, :DC // 2]
    return np.concatenate([cos, sin], axis=-1).astype(f)


def kernel(**inputs):
    import concourse.bacc as _bacc
    from concourse.bass_utils import run_bass_kernel_spmd as _run

    nc = _bacc.Bacc("TRN2", target_bir_lowering=False, num_devices=1)
    given = [(name, np.ascontiguousarray(inputs[name])) for name in _INS] + [("rope_table", rope_table())]
    arrays, args = {}, []
    for name, a in given:
        arrays[f"in_{name}_dram"] = a
        args.append(nc.dram_tensor(f"in_{name}_dram", a.shape, mybir.dt.from_np(a.dtype), kind="ExternalInput").ap())
    args.append(nc.dram_tensor("out_0_dram", (B, S, D), mybir.dt.float32, kind="ExternalOutput").ap())
    xattn_ffn_kernel(nc, *args)
    r = _run(nc, [arrays], core_ids=[0])
    return r.results[0]["out_0_dram"]
```
